# Optimizing a Trainium2 kernel written in Bass

```python
import numpy as np
import jax
import jax.numpy as jnp

def _softmax(x, axis=-1):
    return jax.nn.softmax(x, axis=axis)

def _gelu(x):
    return jax.nn.gelu(x, approximate=True)

def _silu(x):
    return jax.nn.silu(x)

def _sigmoid(x):
    return jax.nn.sigmoid(x)

def _layernorm(x, axis=-1, eps=1e-05):
    m = jnp.mean(x, axis=axis, keepdims=True)
    v = jnp.var(x, axis=axis, keepdims=True)
    return (x - m) / jnp.sqrt(v + eps)

def _scatter_add(tgt, idx, src, axis=0):
    return tgt.at[idx].add(src)

def _segment_sum(src, seg, n):
    return jax.ops.segment_sum(src, seg, n)
kernel_name = 'mk_flamingo_gated_d1_seqx_r4_3c7e83'

def setup_inputs(seed: int=0):
    np.random.seed(seed)
    _w = jnp.asarray

    def _rec_inputs():
        import jax
        import jax.numpy as jnp
        _rk = jax.random.key(seed)
        x = -0.0002928 + 1 * jax.random.normal(jax.random.fold_in(_rk, 1), (16, 512, 256), jnp.float32)
        _lenS = 512 - jax.random.randint(jax.random.fold_in(_rk, 7), (16,), 0, max(1, 512 // 4) + 1, jnp.int32)
        _lenS2 = 1601 - jax.random.randint(jax.random.fold_in(_rk, 8), (16,), 0, max(1, 1601 // 4) + 1, jnp.int32)
        _ctx_1024P = jax.random.normal(jax.random.fold_in(_rk, 11), (16, 16, 256), jnp.float32)
        _ctx_1024c = jax.random.dirichlet(jax.random.fold_in(_rk, 511), 0.3 * jnp.ones((16,), jnp.float32), (16, 1601))
        _ctx_1024t = jnp.einsum('bsk,bkd->bsd', _ctx_1024c, _ctx_1024P)
        _ctx_1024t = _ctx_1024t * jax.lax.rsqrt(jnp.mean(jnp.square(_ctx_1024t)) + 1e-12) * 0.953939
        ctx_1024 = -1.39393e-06 + 0.999914 * (_ctx_1024t + 0.3 * jax.random.normal(jax.random.fold_in(_rk, 611), (16, 1601, 256), jnp.float32))
        _g = jax.random.normal(jax.random.fold_in(_rk, 9001), (2, 1), jnp.float32)
        _g = jnp.sign(_g) * jnp.maximum(jnp.abs(_g), 1.0) + (_g == 0) * 1.0
        g_xattn = _g[0]
        g_ffn = _g[1]
        return (x, ctx_1024, g_xattn, g_ffn)
    x, ctx_1024, g_xattn, g_ffn = _rec_inputs()

    def _L0_xattn_setup():
        import jax, jax.numpy as jnp
        import numpy as np
        import math
        B, T, S, C, H = (2, 512, 512, 256, 16)
        D = C // H

        def _proj_heads(x, W, b):
            y = x @ W.T + b
            Bv, L, _ = y.shape
            return y.reshape(Bv, L, H, D).transpose(0, 2, 1, 3)
        key = jax.random.key(seed)
        ks = jax.random.split(key, 12)
        s = 1.0 / math.sqrt(C)
        inp = {'query': jax.random.normal(ks[0], (B, T, C), jnp.float32), 'key': jax.random.normal(ks[1], (B, S, C), jnp.float32), 'value': jax.random.normal(ks[2], (B, S, C), jnp.float32), 'Wq': jax.random.normal(ks[3], (C, C), jnp.float32) * s, 'bq': jax.random.normal(ks[4], (C,), jnp.float32) * s, 'Wk': jax.random.normal(ks[5], (C, C), jnp.float32) * s, 'bk': jax.random.normal(ks[6], (C,), jnp.float32) * s, 'Wv': jax.random.normal(ks[7], (C, C), jnp.float32) * s, 'bv': jax.random.normal(ks[8], (C,), jnp.float32) * s, 'Wo': jax.random.normal(ks[9], (C, C), jnp.float32) * s, 'bo': jax.random.normal(ks[10], (C,), jnp.float32) * s, 'query_chunk_size': 256}
        return inp
    _L0_xattn_all = _L0_xattn_setup()
    _L0_xattn_in = {k: v for k, v in _L0_xattn_all.items() if k in ('Wq', 'bq', 'Wk', 'bk', 'Wv', 'bv', 'Wo', 'bo')}
    del _L0_xattn_all

    def _L0_ffn_setup():
        import jax, jax.numpy as jnp
        import numpy as np
        E, TOPK, R = (8, 2, 16)
        D, H, GH = (256, 16, 64)
        HD = D // H
        SCALE = HD ** (-0.5)

        def _svd_moe(x, Wm, U, S, V, b, idx, gates):
            main = jnp.einsum('bsd,od->bso', x, Wm)
            Ug, Sg, Vg = (U[idx], S[idx], V[idx])
            xv = jnp.einsum('bsd,bkrd->bksr', x, Vg)
            xvs = xv * Sg[:, :, None, :]
            eo = jnp.einsum('bksr,bkor->bkso', xvs, Ug)
            expert = jnp.einsum('bkso,bk->bso', eo, gates)
            return main + expert + b
        key = jax.random.key(seed)
        ks = jax.random.split(key, 32)
        B, S = (32, 257)
        inp = {'hidden_states': jax.random.normal(ks[0], (B, S, D), jnp.float32)}
        inp['gw1'] = jax.random.normal(ks[1], (GH, D), jnp.float32) * 0.02
        inp['gb1'] = jnp.zeros((GH,), jnp.float32)
        inp['gw2'] = jax.random.normal(ks[2], (E, GH), jnp.float32) * 0.02
        inp['gb2'] = jnp.zeros((E,), jnp.float32)
        i = 3
        for p in ('q', 'k', 'v', 'o'):
            inp[p + 'Wm'] = jax.random.normal(ks[i], (D, D), jnp.float32) * 0.02
            i += 1
            inp[p + 'U'] = jax.random.normal(ks[i], (E, D, R), jnp.float32) * 0.02
            i += 1
            inp[p + 'S'] = jax.random.normal(ks[i], (E, R), jnp.float32) * 0.1
            i += 1
            inp[p + 'V'] = jax.random.normal(ks[i], (E, R, D), jnp.float32) * 0.02
            i += 1
            inp[p + 'b'] = jnp.zeros((D,), jnp.float32)
        return inp
    _L0_ffn_all = _L0_ffn_setup()
    _L0_ffn_in = {k: v for k, v in _L0_ffn_all.items() if k in ('gw1', 'gb1', 'gw2', 'gb2', 'qWm', 'qU', 'qS', 'qV', 'qb', 'kWm', 'kU', 'kS', 'kV', 'kb', 'vWm', 'vU', 'vS', 'vV', 'vb', 'oWm', 'oU', 'oS', 'oV', 'ob')}
    del _L0_ffn_all
    return {'x': x, 'ctx_1024': ctx_1024, 'g_xattn': g_xattn, 'g_ffn': g_ffn, 'L0_xattn_Wq': _L0_xattn_in['Wq'], 'L0_xattn_bq': _L0_xattn_in['bq'], 'L0_xattn_Wk': _L0_xattn_in['Wk'], 'L0_xattn_bk': _L0_xattn_in['bk'], 'L0_xattn_Wv': _L0_xattn_in['Wv'], 'L0_xattn_bv': _L0_xattn_in['bv'], 'L0_xattn_Wo': _L0_xattn_in['Wo'], 'L0_xattn_bo': _L0_xattn_in['bo'], 'L0_ffn_gw1': _L0_ffn_in['gw1'], 'L0_ffn_gb1': _L0_ffn_in['gb1'], 'L0_ffn_gw2': _L0_ffn_in['gw2'], 'L0_ffn_gb2': _L0_ffn_in['gb2'], 'L0_ffn_qWm': _L0_ffn_in['qWm'], 'L0_ffn_qU': _L0_ffn_in['qU'], 'L0_ffn_qS': _L0_ffn_in['qS'], 'L0_ffn_qV': _L0_ffn_in['qV'], 'L0_ffn_qb': _L0_ffn_in['qb'], 'L0_ffn_kWm': _L0_ffn_in['kWm'], 'L0_ffn_kU': _L0_ffn_in['kU'], 'L0_ffn_kS': _L0_ffn_in['kS'], 'L0_ffn_kV': _L0_ffn_in['kV'], 'L0_ffn_kb': _L0_ffn_in['kb'], 'L0_ffn_vWm': _L0_ffn_in['vWm'], 'L0_ffn_vU': _L0_ffn_in['vU'], 'L0_ffn_vS': _L0_ffn_in['vS'], 'L0_ffn_vV': _L0_ffn_in['vV'], 'L0_ffn_vb': _L0_ffn_in['vb'], 'L0_ffn_oWm': _L0_ffn_in['oWm'], 'L0_ffn_oU': _L0_ffn_in['oU'], 'L0_ffn_oS': _L0_ffn_in['oS'], 'L0_ffn_oV': _L0_ffn_in['oV'], 'L0_ffn_ob': _L0_ffn_in['ob']}

def reference(x, ctx_1024, g_xattn, g_ffn, L0_xattn_Wq, L0_xattn_bq, L0_xattn_Wk, L0_xattn_bk, L0_xattn_Wv, L0_xattn_bv, L0_xattn_Wo, L0_xattn_bo, L0_ffn_gw1, L0_ffn_gb1, L0_ffn_gw2, L0_ffn_gb2, L0_ffn_qWm, L0_ffn_qU, L0_ffn_qS, L0_ffn_qV, L0_ffn_qb, L0_ffn_kWm, L0_ffn_kU, L0_ffn_kS, L0_ffn_kV, L0_ffn_kb, L0_ffn_vWm, L0_ffn_vU, L0_ffn_vS, L0_ffn_vV, L0_ffn_vb, L0_ffn_oWm, L0_ffn_oU, L0_ffn_oS, L0_ffn_oV, L0_ffn_ob):
    import jax
    import jax.numpy as jnp

    def _L0_xattn_ref(query, key, value, Wq, bq, Wk, bk, Wv, bv, Wo, bo, query_chunk_size):
        import jax, jax.numpy as jnp
        import numpy as np
        import math
        B, T, S, C, H = (2, 512, 512, 256, 16)
        D = C // H

        def _proj_heads(x, W, b):
            y = x @ W.T + b
            Bv, L, _ = y.shape
            return y.reshape(Bv, L, H, D).transpose(0, 2, 1, 3)
        q = _proj_heads(query, Wq, bq) * (1.0 / math.sqrt(D))
        k = _proj_heads(key, Wk, bk)
        v = _proj_heads(value, Wv, bv)
        scores = jnp.einsum('bhqd,bhkd->bhqk', q, k)
        attn = jax.nn.softmax(scores, axis=-1)
        out = jnp.einsum('bhqk,bhkd->bhqd', attn, v)
        out = out.transpose(0, 2, 1, 3).reshape(query.shape[0], query.shape[1], C)
        return out @ Wo.T + bo

    def _L0_ffn_ref(hidden_states, gw1, gb1, gw2, gb2, qWm, qU, qS, qV, qb, kWm, kU, kS, kV, kb, vWm, vU, vS, vV, vb, oWm, oU, oS, oV, ob):
        import jax, jax.numpy as jnp
        import numpy as np
        E, TOPK, R = (8, 2, 16)
        D, H, GH = (256, 16, 64)
        HD = D // H
        SCALE = HD ** (-0.5)

        def _svd_moe(x, Wm, U, S, V, b, idx, gates):
            main = jnp.einsum('bsd,od->bso', x, Wm)
            Ug, Sg, Vg = (U[idx], S[idx], V[idx])
            xv = jnp.einsum('bsd,bkrd->bksr', x, Vg)
            xvs = xv * Sg[:, :, None, :]
            eo = jnp.einsum('bksr,bkor->bkso', xvs, Ug)
            expert = jnp.einsum('bkso,bk->bso', eo, gates)
            return main + expert + b
        B, S, _ = hidden_states.shape
        pooled = hidden_states.mean(axis=1)
        h = jax.nn.relu(pooled @ gw1.T + gb1)
        logits = h @ gw2.T + gb2
        top_vals, top_idx = jax.lax.top_k(logits, TOPK)
        gates = jax.nn.softmax(top_vals, axis=-1)
        q = _svd_moe(hidden_states, qWm, qU, qS, qV, qb, top_idx, gates) * SCALE
        k = _svd_moe(hidden_states, kWm, kU, kS, kV, kb, top_idx, gates)
        v = _svd_moe(hidden_states, vWm, vU, vS, vV, vb, top_idx, gates)

        def shp(t):
            return t.reshape(B, S, H, HD).transpose(0, 2, 1, 3)
        q, k, v = (shp(q), shp(k), shp(v))
        attn = jax.nn.softmax(jnp.einsum('bhsd,bhtd->bhst', q, k), axis=-1)
        ctx = jnp.einsum('bhst,bhtd->bhsd', attn, v)
        ctx = ctx.transpose(0, 2, 1, 3).reshape(B, S, D)
        out = _svd_moe(ctx, oWm, oU, oS, oV, ob, top_idx, gates)
        return out
    x = x + jnp.tanh(g_xattn[0]) * _L0_xattn_ref(_layernorm(x, axis=-1), ctx_1024, ctx_1024, L0_xattn_Wq, L0_xattn_bq, L0_xattn_Wk, L0_xattn_bk, L0_xattn_Wv, L0_xattn_bv, L0_xattn_Wo, L0_xattn_bo, 256)
    x = x + jnp.tanh(g_ffn[0]) * _L0_ffn_ref(_layernorm(x, axis=-1), L0_ffn_gw1, L0_ffn_gb1, L0_ffn_gw2, L0_ffn_gb2, L0_ffn_qWm, L0_ffn_qU, L0_ffn_qS, L0_ffn_qV, L0_ffn_qb, L0_ffn_kWm, L0_ffn_kU, L0_ffn_kS, L0_ffn_kV, L0_ffn_kb, L0_ffn_vWm, L0_ffn_vU, L0_ffn_vS, L0_ffn_vV, L0_ffn_vb, L0_ffn_oWm, L0_ffn_oU, L0_ffn_oS, L0_ffn_oV, L0_ffn_ob)
    return x

_drawn_inputs = setup_inputs


def setup_inputs(seed=0):
    import zlib

    import numpy as np

    out = dict(_drawn_inputs(seed))
    spreads = {'L0_ffn_gb1': (0.0, 0.8),
     'L0_ffn_gb2': (0.0, 0.8),
     'L0_ffn_qb': (0.0, 0.8),
     'L0_ffn_kb': (0.0, 0.8),
     'L0_ffn_vb': (0.0, 0.328),
     'L0_ffn_ob': (0.0, 0.1)}
    factors = {'L0_xattn_bq': 5.817,
     'L0_xattn_bk': 8.0,
     'L0_ffn_gw1': 8.0,
     'L0_ffn_gw2': 8.0,
     'L0_ffn_qWm': 8.0,
     'L0_ffn_qU': 8.0,
     'L0_ffn_qS': 8.0,
     'L0_ffn_qV': 8.0,
     'L0_ffn_kWm': 8.0,
     'L0_ffn_kU': 8.0,
     'L0_ffn_kS': 8.0,
     'L0_ffn_kV': 8.0,
     'L0_ffn_vU': 8.0,
     'L0_ffn_vS': 8.0,
     'L0_ffn_vV': 8.0,
     'L0_ffn_oU': 8.0,
     'L0_ffn_oS': 8.0,
     'L0_ffn_oV': 8.0}
    for name, (base, spread) in spreads.items():
        noise = np.random.default_rng([zlib.crc32(name.encode()), seed]).standard_normal(out[name].shape)
        drawn = base * np.exp(spread * noise) if base else spread * noise
        out[name] = jnp.asarray(drawn.astype(out[name].dtype))
    for name, factor in factors.items():
        out[name] = (out[name] * factor).astype(out[name].dtype)
    return out
```

```python
from contextlib import ExitStack

import concourse.bass as bass
from concourse import mybir

F32 = mybir.dt.float32
BF16 = mybir.dt.bfloat16
ALU = mybir.AluOpType
ACT = mybir.ActivationFunctionType
AX = mybir.AxisListType

B, T, C = 16, 512, 256
KEYS = 1601
H, D = 16, 16
G, J = 4, 4
QT = T // 128
CC = C // 128
EX, RANK, GH = 8, 16, 64
VW = D + 1
VPAD = J * VW + 32 - VW
EPS = 1e-5
QSCALE = float(D) ** -0.5
TERMS = [(0, 0), (0, 1), (1, 0), (1, 1), (0, 2), (2, 0)]
ROWS = [[0, 16, 32, 48, 64, 80], [64, 80, 96, 112, 0, 16]]
MROW = [96, 32]
KROWS = [99, 128]
TAIL = [("OT", G - 1), ("aT",), ("O",)]
FILL_DMAS = 2 * 2 * len(TERMS)
MROW_DMAS = 2 * 3


def batch_of(b, job):
    if job[0] in ("aT", "O") or job == ("OT", G - 1):
        return b - 1
    if job[0] == "OT" or (job[0] in ("max", "MT") and job[1] > 0):
        return b
    return b + 1


class Stage:

    def __init__(self, cross):
        self.cross = cross
        self.keys = KEYS if cross else T
        self.nk = -(-self.keys // 128)
        self.kr = [min(128, self.keys - 128 * k) for k in range(self.nk)]
        self.nc = -(-self.keys // 512)
        self.cw = [min(512, self.keys - 512 * c) for c in range(self.nc)]
        self.splits = 4 + 4 * self.nc
        self.prologue = self.prep_first() + self.maxima(0)
        self.mid = self.iteration(True, True)
        self.first = self.iteration(False, True)
        self.last = self.iteration(True, False)
        self.loc = {name: self.number(it) for name, it in
                    (("mid", self.mid), ("first", self.first), ("last", self.last))}
        self.loc_pro = {j: n for n, j in enumerate(self.prologue)}
        self.per_iter = len(self.loc["mid"])
        self.n_pro = len(self.prologue)
        assert self.per_iter % 2 == 0 and (self.n_pro + len(self.loc["first"])) % 2 == 0

    def prep_first(self):
        if self.cross:
            return [("xT",), ("Q",)] + [("K", c) for c in range(self.nc)] + [("V", t) for t in range(4)]
        return [("xT",), ("h",), ("lg",), ("gb",), ("W", 0), ("W", 1), ("Q",), ("K", 0), ("V", 0), ("V", 1)]

    def maxima(self, g):
        return [("max", g, hp, qt, c) for hp in range(2) for qt in range(QT) for c in range(self.nc)] + [("MT", g)]

    def iteration(self, post, prep):
        if self.cross:
            extra = [[], [("xT",), ("Q",), ("K", 0), ("K", 1)], [("K", 2), ("K", 3)], [("V", t) for t in range(4)]]
        else:
            extra = [[("xT",), ("h",)], [("lg",), ("gb",), ("W", 0), ("W", 1), ("Q",)],
                     [("K", 0), ("V", 0), ("V", 1)], []]
        out = []
        for g in range(G):
            n = self.nk * J
            slots = [[] for _ in range(n)]
            mx = self.maxima((g + 1) % G) if g < G - 1 or prep else []
            ex = extra[g] if prep else []
            head = [("OT", (g - 1) % G)] if g or post else []
            if g == 0 and post:
                head += [("aT",), ("O",)]
            end = n - 6 if self.cross else n - 5
            for i, job in enumerate(mx):
                lo = 0 if (g < G - 1 or self.cross) else 3
                if g == G - 1 and self.cross:
                    lo = 4
                slots[lo + i * (end - lo) // max(1, len(mx))].append(job)
            if self.cross:
                where = {1: [1, 14, 24, 36], 2: [1, 14], 3: [2, 5, 8, 11]}.get(g, [])
            else:
                where = {0: [10, 14], 1: [1, 3, 6, 8, 11], 2: [0, 2, 4]}.get(g, [])
            for w, job in zip(where, ex):
                slots[w].append(job)
            hw = [9, 14, 20] if self.cross else [6, 8, 10]
            for w, job in zip(hw, head):
                slots[w].insert(0, job)
            out += slots
        return out

    @staticmethod
    def number(slots):
        n, out = 0, {}
        for s in slots:
            for job in s:
                out[job] = n
                n += 1
        return out

    def base(self, b):
        if isinstance(b, int) and b == 0:
            return self.n_pro
        return b * self.per_iter + (self.n_pro + len(self.loc["first"]) - self.per_iter)

    def kind(self, b):
        if isinstance(b, int):
            return {0: "first", B - 1: "last"}.get(b, "mid")
        return "mid"

    def at(self, b, job):
        return self.base(b) + self.loc[self.kind(b)][job]

    def slot(self, b, job):
        n = self.loc[self.kind(b)][job]
        return (n + self.n_pro) % 2 if isinstance(b, int) and b == 0 else n % 2

    def before(self, b, job):
        if isinstance(b, int) and b == 0:
            return self.loc_pro[job]
        return self.base(b) + (self.loc["mid"][job] - self.per_iter)


def run_stage(nc, st, sems, x_in, x_out, ctxT, w, tag):
    cross, NK, NC, KR, CW = st.cross, st.nk, st.nc, st.kr, st.cw
    NT = J * NK
    STEPS = G * NK
    NV = 4 if cross else 2
    VT = 4 if cross else 2
    ctx = ExitStack()
    with ctx:
        def sb(name, shape, dt=F32):
            return ctx.enter_context(nc.sbuf_tensor(f"{tag}_{name}", shape, dt))

        def sem(name):
            return sems.enter_context(nc.semaphore(f"{tag}_{name}"))

        ring = [ctx.enter_context(nc.psum_tensor(f"{tag}_ring{i}", [128, 2, 512], F32)) for i in range(2)]
        score = [ctx.enter_context(nc.psum_tensor(f"{tag}_score{i}", [128, 512], F32)) for i in range(3)]
        heads = ctx.enter_context(nc.psum_tensor(f"{tag}_heads", [128, 512], F32))

        xt = sb("xt", [128, QT, C])
        xT = sb("xT", [128, CC, T])
        xres = sb("xres", [128, QT, C])
        xo = sb("xo", [128, QT, C])
        qf = sb("qf", [128, CC, T])
        kf = [sb(f"kf{i}", [128, CC, 512]) for i in range(2)]
        rest = sb("rest", [128, CC, 512])
        qp = sb("qp", [128, 3, CC, T], BF16)
        kp = sb("kp", [128, 3, CC, st.keys], BF16)
        kst = sb("kst", [128, G, J, st.keys], BF16)
        qst = sb("qst", [128, G, J, T], BF16)
        vs = sb("vs", [128, NK, C])
        vp = [sb(f"vp{i}", [128, NK, VPAD]) for i in range(2)]
        prob = [sb(f"prob{i}", [128, J, T]) for i in range(2)]
        hsb = sb("hsb", [128, T])
        attn = sb("attn", [128, QT, C])
        attnT = sb("attnT", [128, CC, T])
        rden = sb("rden", [128, QT, J])
        stats = sb("stats", [128, QT, 6])
        mv = sb("mv", [128, QT, 2])
        veps = sb("veps", [128, QT])
        nmean = sb("nmean", [128, QT])
        rstd = sb("rstd", [128, QT])
        nhalf = sb("nhalf", [128, QT])
        mxp = sb("mxp", [128, 2, 2, QT, NC])
        negm = sb("negm", [128, 2, 2 * QT])
        mrest = sb("mrest", [128, 2, 2 * QT])
        mparts = sb("mparts", [128, 2, 3, 2 * QT], BF16)
        mT = sb("mT", [48, 128], BF16)
        ident = sb("ident", [128, 128])
        identb = sb("identb", [128, 128], BF16)
        bq = sb("bq", [128, CC])
        bk = sb("bk", [128, CC])
        bv = sb("bv", [128, C])
        bo = sb("bo", [128, C])
        gate = sb("gate", [128, 1])
        weights = ["q", "k", "v", "o"]
        if cross:
            cT = sb("cT", [128, CC, KEYS])
            wT = {n: sb(f"w{n}", [128, CC, C]) for n in weights}
        else:
            cT = xT
            wall = sb("wall", [128, 4, CC, C])
            wT = {n: wall[:, i] for i, n in enumerate(weights)}
            wT["o"] = sb("wo_now", [128, CC, C])
            wm = sb("wm", [128, 4, CC, C])
            uT = sb("uT", [128, 4, C])
            vw = sb("vw", [128, 4, C])
            uc = sb("uc", [128, 4, C])
            sv = sb("sv", [128, 4])
            coef = sb("coef", [128, 4])
            gw1 = sb("gw1", [128, CC, GH])
            gw2 = sb("gw2", [GH, EX])
            gb1 = sb("gb1", [GH, 1])
            gb2 = sb("gb2", [1, EX])
            prio = sb("prio", [1, EX])
            onehot = sb("onehot", [128, EX])
            ones = sb("ones", [1, 128])
            euler = sb("euler", [1, 1])
            pool_s = sb("pool_s", [128, CC])
            pooled = sb("pooled", [128, CC])
            hid = sb("hid", [GH, 1])
            lg = sb("lg", [1, EX])
            lg2 = sb("lg2", [1, EX])
            top = sb("top", [1, 8])
            cand = sb("cand", [1, 2, EX])
            pick = sb("pick", [1, 2, EX])
            gates = sb("gates", [1, 2, EX])
            gsel = sb("gsel", [128, EX])
            csum = sb("csum", [128, 1])

        pool_past, sp_past, dve_past, pe_past = (sem(f"{e}_past") for e in ("pool", "sp", "dve", "pe"))
        w_loaded = sem("w_loaded")
        const_dve = sem("const_dve")
        const_pool = sem("const_pool")
        gate_tanh = sem("gate_tanh")
        x_loaded = sem("x_loaded")
        ctx_loaded = sem("ctx_loaded")
        xres_loaded = sem("xres_loaded")
        fill_done = [sem(f"fill_done{g}") for g in range(G)]
        mrow_done = sem("mrow_done")
        stored = sem("stored")
        ring_full = sem("ring_full")
        ring_free = sem("ring_free")
        score_full = sem("score_full")
        exp_done = sem("exp_done")
        pv_done = sem("pv_done")
        heads_copied = sem("heads_copied")
        stats_done = sem("stats_done")
        stats_step = sem("stats_step")
        ln_step = sem("ln_step")
        xhat_ready = sem("xhat_ready")
        xb_ready = sem("xb_ready")
        split = sem("split")
        v_packed = sem("v_packed")
        m_step = sem("m_step")
        den_ready = sem("den_ready")
        if not cross:
            gate_step = sem("gate_step")
            gate_exp = sem("gate_exp")
            uc_ready = sem("uc_ready")
            wo_kept = sem("wo_kept")
        GATE_STEPS = 19
        CONST_DVE, CONST_POOL = (6, 7) if cross else (7, 12 + EX)
        block = ctx.enter_context(nc.Block())

        x_rows = x_in.rearrange("b (p t) c -> b p t c", t=QT)
        out_rows = x_out.rearrange("b (p t) c -> b p t c", t=QT)
        n_weights = 9 if cross else 16

        def over_batches(engine, body):
            body(0)
            with engine.Fori(1, B - 1) as b:
                body(b)
            body(B - 1)

        def flags(b):
            return (not (isinstance(b, int) and b == 0), not (isinstance(b, int) and b == B - 1))

        END = st.base(B - 1) + len(st.loc["last"])

        def in_tail(job):
            return END + TAIL.index(job)

        NEEDS = {"aT": ("OT", G - 1), "O": ("aT",), "Q": ("xT",) if cross else ("W", 1), "lg": ("h",)}

        @block.sync
        def _(sp):
            loads = []
            if cross:
                loads += [(wT[n][:], w["w" + n].rearrange("(c p) o -> p c o", p=128)) for n in weights]
                loads += [(bo[:], w["bo"]), (bv[:], w["bv"]), (bq[:], w["bq"]), (bk[:], w["bk"]), (gate[:], w["gate"])]
            else:
                loads += [(wm[:, i], w["w" + n].rearrange("(c p) o -> p c o", p=128)) for i, n in enumerate(weights)]
                loads += [(uT[:], w["u"].rearrange("n p o -> p n o")), (vw[:], w["v"].rearrange("n p o -> p n o")),
                          (sv[:], w["s"]), (bo[:], w["bo"]), (bv[:], w["bv"]), (bq[:], w["bq"]), (bk[:], w["bk"]),
                          (gate[:], w["gate"]), (gw1[:], w["gw1"].rearrange("(c p) o -> p c o", p=128)),
                          (gw2[:], w["gw2"]), (gb1[:], w["gb1"]), (gb2[:], w["gb2"])]
            assert len(loads) == n_weights
            sp.dma_start(xt[:], x_rows[0]).then_inc(x_loaded, 16)
            if cross:
                sp.dma_start(cT[:], ctxT[0].rearrange("(c p) k -> p c k", p=128)).then_inc(ctx_loaded, 16)
            for dst, src in loads:
                sp.dma_start(dst, src).then_inc(w_loaded, 16)

            def fill(b, g):
                first = isinstance(b, int) and b == 0
                sp.wait_ge(split, (b + 1) * st.splits)
                sp.sem_inc(sp_past, 1)
                if not first:
                    sp.wait_ge(score_full, b * (G * NT) + ((g + 1 - G) * NT))
                for e in range(2):
                    for (tq, tk), row in zip(TERMS, ROWS[e]):
                        for parts, stack, t in ((qp, qst, tq), (kp, kst, tk)):
                            sp.dma_start(
                                stack[row:row + D, g, 2 * e:2 * e + 2, :],
                                parts[(2 * g + e) * D:(2 * g + e + 1) * D, t, :, :]).then_inc(fill_done[g], 16)

            def max_rows(job_number, g):
                sp.wait_ge(ring_free, job_number + 1)
                for e in range(2):
                    for part in range(3):
                        sp.dma_start(
                            qst[MROW[e] + part:MROW[e] + part + 1, g, 2 * e:2 * e + 2, :]
                            .rearrange("o h (t p) -> o (h t) p", p=128),
                            mT[24 * e + 8 * part:24 * e + 8 * part + 8, :]).then_inc(mrow_done, 16)

            for g in range(3):
                fill(0, g)
            max_rows(st.loc_pro[("MT", 0)], 0)

            def body(b):
                post, prep = flags(b)
                fill(b, 3)
                if prep:
                    sp.wait_ge(ring_free, st.before(b, ("xT",)) + 1)
                    sp.dma_start(xt[:], x_rows[b + 1]).then_inc(x_loaded, 16)
                    if cross:
                        sp.wait_ge(ring_free, st.before(b, ("V", NV - 1)) + 1)
                        sp.dma_start(cT[:], ctxT[b + 1].rearrange("(c p) k -> p c k", p=128)).then_inc(ctx_loaded, 16)
                if post:
                    if not isinstance(b, int) or b > 1:
                        sp.wait_ge(ring_free, st.before(b, ("O",)) + 1)
                    sp.dma_start(xres[:], x_rows[b - 1]).then_inc(xres_loaded, 16)
                    sp.wait_ge(ring_free, st.at(b, ("O",)) + 1)
                    sp.dma_start(out_rows[b - 1], xo[:]).then_inc(stored, 16)
                max_rows(st.at(b, ("MT", 1)), 1)
                max_rows(st.at(b, ("MT", 2)), 2)
                if prep:
                    fill(b + 1, 0)
                max_rows(st.at(b, ("MT", 3)), 3)
                if prep:
                    fill(b + 1, 1)
                    fill(b + 1, 2)
                    max_rows(st.at(b, ("MT", 0)), 0)

            over_batches(sp, body)
            sp.wait_ge(ring_free, st.at(B - 1, ("O",)) + 1)
            sp.dma_start(xres[:], x_rows[B - 1]).then_inc(xres_loaded, 16)
            sp.wait_ge(ring_free, END + 3)
            sp.dma_start(out_rows[B - 1], xo[:]).then_inc(stored, 16)
            sp.wait_ge(stored, 16 * B)

        @block.tensor
        def _(pe):
            def ring_job(b, job, base, loc, slot):
                n, kind = base + loc[job], job[0]
                after = NEEDS.get(kind)
                if not isinstance(n, int) or n >= 2 or after:
                    pe.wait_ge(ring_free, base + max(loc[job] - 1, loc[after] + 1 if after else 0))
                if kind == "lg":
                    pe.sem_inc(pe_past, 1)
                if kind == "max":
                    _, g, hp, qt, c = job
                    pe.wait_ge(fill_done[g], b * (FILL_DMAS * 16) + FILL_DMAS * 16)
                    for e in range(2):
                        j, r = 2 * e + hp, 64 * e
                        mm = pe.matmul(slot[:, e, 0:CW[c]], qst[r:r + 64, g, j, 128 * qt:128 * qt + 128],
                                       kst[r:r + 64, g, j, 512 * c:512 * c + CW[c]], start=True, stop=True)
                elif kind == "MT":
                    pe.wait_ge(m_step, b * (5 * G) + 5 * (job[1] + 1))
                    pe.sem_inc(pe_past, 1)
                    mm = pe.transpose(slot[0:48, 0, 0:64].bitcast(BF16), mparts[:].rearrange("p e t q -> p (e t q)"),
                                      identb[:])
                elif kind == "OT":
                    pe.wait_ge(heads_copied, b * G + job[1] + 1)
                    for qt in range(QT):
                        mm = pe.transpose(slot[:, 0, 128 * qt:128 * qt + 128], hsb[:, 128 * qt:128 * qt + 128], ident[:])
                elif kind in ("aT", "xT"):
                    src = attn if kind == "aT" else xt
                    if kind == "xT":
                        pe.wait_ge(xhat_ready, b + 1)
                    for c in range(CC):
                        for qt in range(QT):
                            mm = pe.transpose(slot[:, c, 128 * qt:128 * qt + 128],
                                              src[:, qt, 128 * c:128 * c + 128], ident[:])
                elif kind == "O":
                    if not cross:
                        pe.wait_ge(wo_kept, b + 1)
                    for qt in range(QT):
                        for c in range(CC):
                            mm = pe.matmul(slot[:, qt // 2, 256 * (qt % 2):256 * (qt % 2) + 256],
                                           attnT[:, c, 128 * qt:128 * qt + 128], wT["o"][:, c, :],
                                           start=(c == 0), stop=(c == CC - 1))
                elif kind == "Q":
                    for m in range(CC):
                        for c in range(CC):
                            mm = pe.matmul(slot[:, m, :], wT["q"][:, c, 128 * m:128 * m + 128], xT[:, c, :],
                                           start=(c == 0), stop=(c == CC - 1))
                elif kind == "K":
                    k = job[1]
                    if cross:
                        pe.wait_ge(ctx_loaded, b * 16 + 16)
                    for m in range(CC):
                        for c in range(CC):
                            mm = pe.matmul(slot[:, m, 0:CW[k]], wT["k"][:, c, 128 * m:128 * m + 128],
                                           cT[:, c, 512 * k:512 * k + CW[k]], start=(c == 0), stop=(c == CC - 1))
                elif kind == "V":
                    for i, kt in enumerate(range(VT * job[1], min(NK, VT * (job[1] + 1)))):
                        for c in range(CC):
                            mm = pe.matmul(slot[0:KR[kt], i // 2, 256 * (i % 2):256 * (i % 2) + 256],
                                           cT[:, c, 128 * kt:128 * kt + KR[kt]], wT["v"][:, c, :],
                                           start=(c == 0), stop=(c == CC - 1))
                elif kind == "h":
                    pe.wait_ge(gate_step, b * GATE_STEPS + 2)
                    for c in range(CC):
                        mm = pe.matmul(slot[0:GH, 0, 0:1], gw1[:, c, :], pooled[:, c:c + 1],
                                       start=(c == 0), stop=(c == CC - 1))
                elif kind == "lg":
                    mm = pe.matmul(slot[0:1, 0, 0:EX], hid[:], gw2[:], start=True, stop=True)
                elif kind == "gb":
                    pe.wait_ge(gate_step, b * GATE_STEPS + 17)
                    mm = pe.matmul(slot[:, 0, 0:EX], ones[:], gates[:, 1, :], start=True, stop=True)
                elif kind == "W":
                    pe.wait_ge(uc_ready, b + 1)
                    for i in range(2):
                        for c in range(CC):
                            mm = pe.matmul(slot[:, i, 256 * c:256 * c + 256],
                                           vw[:, 2 * job[1] + i, 128 * c:128 * c + 128], uc[:, 2 * job[1] + i, :],
                                           start=True, stop=True)
                mm.then_inc(ring_full, 1)

            def score_tile(b, g, kt, j):
                i = (g * NK + kt) * J + j
                n = b * (G * NT) + i
                last = i - 3 if i >= 3 else [x for x in range(G * NT) if x % 3 == i % 3][-1] - G * NT
                if not (isinstance(b, int) and b == 0 and last < 0):
                    pe.wait_ge(exp_done, b * (G * NT) + last + 1)
                if kt == 0 and j == 0:
                    pe.wait_ge(mrow_done, b * (G * MROW_DMAS * 16) + (g + 1) * MROW_DMAS * 16)
                rows = KROWS[j // 2]
                pe.matmul(score[i % 3][0:KR[kt], :], kst[0:rows, g, j, 128 * kt:128 * kt + KR[kt]],
                          qst[0:rows, g, j, :], start=True, stop=True).then_inc(score_full, 1)

            def pv_step(b, g, kt):
                s = g * NK + kt
                pe.wait_ge(exp_done, b * (G * NT) + J * (s + 1))
                if kt == 0:
                    pe.wait_ge(v_packed, b * G + g + 1)
                    if not (isinstance(b, int) and b == 0 and g == 0):
                        pe.wait_ge(heads_copied, b * G + g)
                for j in range(J):
                    mm = pe.matmul(heads[32 * j:32 * j + 32, :], vp[g % 2][0:KR[kt], kt, VW * j:VW * j + 32],
                                   prob[s % 2][0:KR[kt], j, :], start=(kt == 0), stop=(kt == NK - 1))
                mm.then_inc(pv_done, 1)

            pe.wait_ge(w_loaded, 16 * n_weights)
            pe.wait_ge(const_dve, CONST_DVE)
            pe.wait_ge(const_pool, CONST_POOL)
            for n, job in enumerate(st.prologue):
                ring_job(0, job, 0, st.loc_pro, ring[n % 2])

            def body(b):
                post, prep = flags(b)
                jobs = {"first": st.first, "mid": st.mid, "last": st.last}[st.kind(b)]
                i = 0
                for g in range(G):
                    for kt in range(NK):
                        for j in range(J):
                            for job in jobs[i]:
                                ring_job(batch_of(b, job), job, st.base(b), st.loc[st.kind(b)],
                                         ring[st.slot(b, job)])
                            score_tile(b, g, kt, j)
                            i += 1
                        s = g * NK + kt - 1
                        if s >= 0:
                            pv_step(b, s // NK, s % NK)
                        elif post:
                            pv_step(b - 1, G - 1, NK - 1)

            over_batches(pe, body)
            pv_step(B - 1, G - 1, NK - 1)
            for i, job in enumerate(TAIL):
                ring_job(B - 1, job, END, {other: k for k, other in enumerate(TAIL)}, ring[(END + i) % 2])

        @block.scalar
        def _(act):
            act.wait_ge(w_loaded, 16 * n_weights)
            act.activation(gate[:], gate[:], ACT.Tanh).then_inc(gate_tanh, 1)

            def exp_tile(b, g, kt, j):
                s = g * NK + kt
                act.wait_ge(score_full, b * (G * NT) + J * s + j + 1)
                if j == 0 and not (isinstance(b, int) and b == 0 and s < 2):
                    act.wait_ge(pv_done, b * STEPS + s - 1)
                i = J * s + j
                act.activation(prob[s % 2][0:KR[kt], j, :], score[i % 3][0:KR[kt], :], ACT.Exp).then_inc(exp_done, 1)

            def copy_heads(b, g, last_ot):
                act.wait_ge(pv_done, b * STEPS + (g + 1) * NK)
                if last_ot is not None:
                    act.wait_ge(ring_full, last_ot + 1)
                act.activation(hsb[:], heads[:], ACT.Copy).then_inc(heads_copied, 1)

            def body(b):
                post, _ = flags(b)
                for g in range(G):
                    for kt in range(NK):
                        for j in range(J):
                            exp_tile(b, g, kt, j)
                        if kt == 0 and g == 0 and post:
                            copy_heads(b - 1, G - 1, st.before(b, ("OT", 2)))
                        elif kt == 0 and g > 0:
                            prev = ("OT", (g - 2) % G)
                            copy_heads(b, g - 1, None if g == 1 and not post else st.at(b, prev))

            over_batches(act, body)
            copy_heads(B - 1, G - 1, st.at(B - 1, ("OT", 2)))

        @block.vector
        def _(dve):
            dve.memset(vs[:], 0.0).then_inc(const_dve, 1)
            dve.memset(vp[0][:], 1.0).then_inc(const_dve, 1)
            dve.memset(vp[1][:], 1.0).then_inc(const_dve, 1)
            dve.wait_ge(const_pool, CONST_POOL)
            dve.tensor_copy(identb[:], ident[:]).then_inc(const_dve, 1)
            dve.wait_ge(gate_tanh, 1)
            dve.tensor_scalar(bo[:], bo[:], gate[:], None, ALU.mult).then_inc(const_dve, 1)
            if cross:
                dve.tensor_scalar(wT["o"][:], wT["o"][:], gate[:], None, ALU.mult).then_inc(const_dve, 1)
            else:
                dve.tensor_scalar(wm[:, 3], wm[:, 3], gate[:], None, ALU.mult).then_inc(const_dve, 1)
                dve.tensor_scalar(sv[:, 3:4], sv[:, 3:4], gate[:], None, ALU.mult).then_inc(const_dve, 1)
            dve.wait_ge(const_dve, CONST_DVE)

            def layernorm_stats(b):
                dve.wait_ge(x_loaded, b * 16 + 16)
                if not isinstance(b, int) or b > 0:
                    dve.wait_ge(xhat_ready, b)
                for qt in range(QT):
                    last = dve.bn_stats(stats[:, qt, :], xt[:, qt, :])
                last.then_inc(stats_step, 1)
                dve.wait_ge(stats_step, b + 1)
                dve.sem_inc(dve_past, 1)
                for qt in range(QT):
                    last = dve.bn_aggr(mv[:, qt, :], stats[:, qt, :])
                last.then_inc(stats_done, 1)

            def ring_job(b, job, number, slot):
                n, kind = number(job), job[0]
                if kind == "MT":
                    g = job[1]
                    k = b * (5 * G) + 5 * g
                    dve.wait_ge(ring_free, n)
                    dve.tensor_reduce(negm[:], mxp[:].rearrange("p e h q c -> p e (h q) c"), AX.X, ALU.max,
                                      negate=True).then_inc(m_step, 1)
                    dve.wait_ge(m_step, k + 1)
                    dve.tensor_copy(mparts[:, :, 0, :], negm[:]).then_inc(m_step, 1)
                    dve.wait_ge(m_step, k + 2)
                    dve.tensor_tensor(mrest[:], negm[:], mparts[:, :, 0, :], ALU.subtract).then_inc(m_step, 1)
                    dve.wait_ge(m_step, k + 3)
                    dve.tensor_copy(mparts[:, :, 1, :], mrest[:]).then_inc(m_step, 1)
                    dve.wait_ge(m_step, k + 4)
                    dve.tensor_tensor(mparts[:, :, 2, :], mrest[:], mparts[:, :, 1, :], ALU.subtract).then_inc(m_step, 1)
                    if not (isinstance(b, int) and b == 0 and g == 0):
                        dve.wait_ge(mrow_done, b * (G * MROW_DMAS * 16) + g * MROW_DMAS * 16)
                if kind == "OT":
                    dve.wait_ge(ring_free, n)
                if kind == "K":
                    if job[1] >= 2:
                        dve.wait_ge(split, b * st.splits + 4 + 4 * (job[1] - 2) + 2)
                    elif not (isinstance(b, int) and b == 0):
                        dve.wait_ge(split, b * st.splits)
                if kind == "Q" and not (isinstance(b, int) and b == 0):
                    dve.wait_ge(split, b * st.splits)
                if kind == "V" and job[1] == 0 and not (isinstance(b, int) and b == 0):
                    dve.wait_ge(v_packed, b * G)
                if kind == "O":
                    dve.wait_ge(xb_ready, b + 1)
                    if not (isinstance(b, int) and b == 0):
                        dve.wait_ge(stored, b * 16)
                if kind == "W" and job[1] == 1 and not (isinstance(b, int) and b == 0):
                    dve.wait_ge(wo_kept, b)
                dve.wait_ge(ring_full, n + 1)
                if kind == "max":
                    _, g, hp, qt, c = job
                    op = dve.tensor_reduce(mxp[:, :, hp, qt, c], slot[:, :, 0:CW[c]], AX.X, ALU.max)
                elif kind == "MT":
                    op = dve.tensor_copy(mT[:], slot[0:48, 0, 0:64].bitcast(BF16))
                elif kind == "OT":
                    g = job[1]
                    seen = slot[:, 0, :].rearrange("p (q j d) -> p q j d", q=QT, j=J)
                    dve.reciprocal(rden[:], seen[:, :, :, D]).then_inc(den_ready, 1)
                    dve.wait_ge(den_ready, b * G + g + 1)
                    op = dve.tensor_tensor(
                        attn[:, :, D * J * g:D * J * (g + 1)].rearrange("p q (j d) -> p q j d", j=J),
                        seen[:, :, :, 0:D], rden[:].unsqueeze(3).broadcast_to([128, QT, J, D]), ALU.mult)
                elif kind == "aT":
                    op = dve.tensor_copy(attnT[:], slot[:])
                elif kind == "xT":
                    op = dve.tensor_copy(xT[:], slot[:])
                elif kind == "O":
                    op = dve.tensor_tensor(xo[:].rearrange("p q c -> p (q c)"), xres[:].rearrange("p q c -> p (q c)"),
                                           slot[:].rearrange("p a n -> p (a n)"), ALU.add)
                elif kind == "Q":
                    for m in range(CC):
                        op = dve.tensor_scalar(qf[:, m, :], slot[:, m, :], bq[:, m:m + 1], QSCALE, ALU.add, ALU.mult)
                elif kind == "K":
                    c = job[1]
                    for m in range(CC):
                        op = dve.tensor_scalar(kf[c % 2][:, m, 0:CW[c]], slot[:, m, 0:CW[c]], bk[:, m:m + 1], None, ALU.add)
                elif kind == "V":
                    k0, k1 = VT * job[1], min(NK, VT * (job[1] + 1))
                    kr = KR[k1 - 1]
                    op = dve.tensor_tensor(
                        vs[0:kr, k0:k1, :],
                        slot[0:kr].rearrange("p a (b n) -> p (a b) n", n=C)[:, 0:k1 - k0, :],
                        bv[0:kr].unsqueeze(1).broadcast_to([kr, k1 - k0, C]), ALU.add)
                elif kind == "h":
                    op = dve.tensor_scalar(hid[:], slot[0:GH, 0, 0:1], gb1[:], 0.0, ALU.add, ALU.max)
                elif kind == "lg":
                    op = dve.tensor_tensor(lg[:], gb2[:], slot[0:1, 0, 0:EX], ALU.add)
                elif kind == "gb":
                    op = dve.tensor_tensor(gsel[:], onehot[:], slot[:, 0, 0:EX], ALU.mult)
                elif kind == "W":
                    i = 2 * job[1]
                    op = dve.tensor_tensor(wall[:, i:i + 2].rearrange("p i c n -> p (i c n)"),
                                           wm[:, i:i + 2].rearrange("p i c n -> p (i c n)"),
                                           slot[:].rearrange("p a n -> p (a n)"), ALU.add)
                op.then_inc(ring_free, 1)
                if not cross and kind == "xT":
                    k = b * GATE_STEPS
                    dve.wait_ge(ring_free, n + 1)
                    dve.tensor_reduce(pool_s[:], xT[:], AX.X, ALU.add).then_inc(gate_step, 1)
                    dve.wait_ge(gate_step, k + 1)
                    dve.tensor_scalar(pooled[:], pool_s[:], 1.0 / T, None, ALU.mult).then_inc(gate_step, 1)
                if kind == "lg":
                    choose(b, n)
                if kind == "gb":
                    k = b * GATE_STEPS
                    dve.wait_ge(ring_free, n + 1)
                    dve.tensor_reduce(csum[:], gsel[:], AX.X, ALU.add).then_inc(gate_step, 1)
                    dve.wait_ge(gate_step, k + 18)
                    dve.tensor_scalar(coef[:], sv[:], csum[:], None, ALU.mult).then_inc(gate_step, 1)

            def choose(b, n):
                k = [b * GATE_STEPS + 2]

                def done(op):
                    op.then_inc(gate_step, 1)
                    k[0] = k[0] + 1
                    dve.wait_ge(gate_step, k[0])

                dve.wait_ge(ring_free, n + 1)
                for r, row in ((0, lg), (1, lg2)):
                    if r:
                        done(dve.scalar_tensor_tensor(lg2[:], pick[:, 0, :], -3.0e38, lg[:], ALU.mult, ALU.add))
                    done(dve.tensor_reduce(top[:, 2 * r:2 * r + 1], row[:], AX.X, ALU.max))
                    done(dve.scalar_tensor_tensor(cand[:, r, :], row[:], top[:, 2 * r:2 * r + 1], prio[:],
                                                  ALU.is_ge, ALU.mult))
                    done(dve.tensor_reduce(top[:, 2 * r + 1:2 * r + 2], cand[:, r, :], AX.X, ALU.max))
                    done(dve.tensor_scalar(pick[:, r, :], cand[:, r, :], top[:, 2 * r + 1:2 * r + 2], None, ALU.is_equal))
                done(dve.tensor_tensor(top[:, 4:5], top[:, 2:3], top[:, 0:1], ALU.subtract))
                dve.wait_ge(gate_exp, b + 1)
                done(dve.tensor_scalar(top[:, 6:7], top[:, 5:6], 1.0, None, ALU.add))
                done(dve.reciprocal(top[:, 7:8], top[:, 6:7]))
                done(dve.tensor_scalar(gates[:, 0, :], pick[:, 1, :], top[:, 5:6], None, ALU.mult))
                done(dve.tensor_tensor(gates[:, 0, :], gates[:, 0, :], pick[:, 0, :], ALU.add))
                done(dve.tensor_scalar(gates[:, 1, :], gates[:, 0, :], top[:, 7:8], None, ALU.mult))

            layernorm_stats(0)
            for n, job in enumerate(st.prologue):
                ring_job(0, job, st.loc_pro.get, ring[n % 2])

            def body(b):
                post, prep = flags(b)
                jobs = {"first": st.first, "mid": st.mid, "last": st.last}[st.kind(b)]
                if prep:
                    layernorm_stats(b + 1)
                for i, here in enumerate(jobs):
                    for job in here:
                        ring_job(batch_of(b, job), job, lambda other: st.at(b, other), ring[st.slot(b, job)])

            over_batches(dve, body)
            for i, job in enumerate(TAIL):
                ring_job(B - 1, job, in_tail, ring[(END + i) % 2])

        @block.gpsimd
        def _(pool):
            pool.memset(ident[:], 0.0).then_inc(const_pool, 1)
            pool.wait_ge(const_pool, 1)
            pool.affine_select(out=ident[:], in_=ident[:], compare_op=ALU.not_equal, fill=1.0, base=0,
                               pattern=[[-1, 128]], channel_multiplier=1).then_inc(const_pool, 1)
            pool.wait_ge(const_pool, 2)
            pool.memset(kst[96:128, :, 0:2, :], 1.0).then_inc(const_pool, 1)
            pool.wait_ge(const_pool, 3)
            pool.memset(kst[32:64, :, 2:4, :], 0.0).then_inc(const_pool, 1)
            pool.wait_ge(const_pool, 4)
            pool.memset(qst[32:64, :, 2:4, :], 0.0).then_inc(const_pool, 1)
            pool.wait_ge(const_pool, 5)
            pool.memset(kst[32:35, :, 2:4, :], 1.0).then_inc(const_pool, 1)
            pool.wait_ge(const_pool, 6)
            pool.memset(nhalf[:], -0.5).then_inc(const_pool, 1)
            pool.wait_ge(const_pool, 7)
            if not cross:
                for e in range(EX):
                    pool.memset(prio[:, e:e + 1], float(EX - e)).then_inc(const_pool, 1)
                    pool.wait_ge(const_pool, 8 + e)
                pool.memset(ones[:], 1.0).then_inc(const_pool, 1)
                pool.wait_ge(const_pool, 8 + EX)
                pool.memset(euler[:], 2.718281828459045).then_inc(const_pool, 1)
                pool.wait_ge(const_pool, 9 + EX)
                pool.memset(onehot[:], 1.0).then_inc(const_pool, 1)
                pool.wait_ge(const_pool, 10 + EX)
                pool.affine_select(out=onehot[:], in_=onehot[:], compare_op=ALU.is_ge, fill=0.0, base=0,
                                   pattern=[[-RANK, EX]], channel_multiplier=1).then_inc(const_pool, 1)
                pool.wait_ge(const_pool, 11 + EX)
                pool.affine_select(out=onehot[:], in_=onehot[:], compare_op=ALU.is_ge, fill=0.0, base=RANK - 1,
                                   pattern=[[RANK, EX]], channel_multiplier=-1).then_inc(const_pool, 1)
            pool.wait_ge(const_pool, CONST_POOL)
            pool.wait_ge(const_dve, CONST_DVE)

            def layernorm(b):
                k = b * 3
                pool.wait_ge(stats_done, b + 1)
                pool.sem_inc(pool_past, 1)
                pool.tensor_scalar(veps[:], mv[:, :, 1], EPS, None, ALU.add).then_inc(ln_step, 1)
                pool.tensor_scalar(nmean[:], mv[:, :, 0], -1.0, None, ALU.mult).then_inc(ln_step, 1)
                pool.wait_ge(ln_step, k + 2)
                pool.sem_inc(pool_past, 1)
                pool.tensor_tensor(rstd[:], veps[:], nhalf[:], ALU.pow).then_inc(ln_step, 1)
                pool.wait_ge(ln_step, k + 3)
                pool.sem_inc(pool_past, 1)
                for qt in range(QT):
                    last = pool.tensor_scalar(xt[:, qt, :], xt[:, qt, :], nmean[:, qt:qt + 1], rstd[:, qt:qt + 1],
                                              ALU.add, ALU.mult)
                last.then_inc(xhat_ready, 1)

            def split_parts(b, src, parts, cols, k, evacuated):
                pool.wait_ge(ring_free, evacuated + 1)
                pool.sem_inc(pool_past, 1)
                n = b * st.splits + k
                r = rest[:, :, 0:src.shape[2]]
                pool.tensor_copy(parts[:, 0, :, cols], src).then_inc(split, 1)
                pool.wait_ge(split, n + 1)
                pool.sem_inc(pool_past, 1)
                pool.tensor_tensor(r, src, parts[:, 0, :, cols], ALU.subtract).then_inc(split, 1)
                pool.wait_ge(split, n + 2)
                pool.sem_inc(pool_past, 1)
                pool.tensor_copy(parts[:, 1, :, cols], r).then_inc(split, 1)
                pool.wait_ge(split, n + 3)
                pool.sem_inc(pool_past, 1)
                pool.tensor_tensor(parts[:, 2, :, cols], r, parts[:, 1, :, cols], ALU.subtract).then_inc(split, 1)
                pool.wait_ge(split, n + 4)
                pool.sem_inc(pool_past, 1)

            def split_q(b, number):
                if not (isinstance(b, int) and b == 0):
                    for g in range(G):
                        pool.wait_ge(fill_done[g], b * (FILL_DMAS * 16))
                        pool.sem_inc(pool_past, 1)
                split_parts(b, qf[:], qp, slice(0, T), 0, number(("Q",)))

            def split_k(b, c, number):
                split_parts(b, kf[c % 2][:, :, 0:CW[c]], kp, slice(512 * c, 512 * c + CW[c]), 4 + 4 * c,
                            number(("K", c)))

            def pack_v(b, g, number):
                if number is not None:
                    pool.wait_ge(ring_free, number(("V", NV - 1)) + 1)
                    pool.sem_inc(pool_past, 1)
                if not (isinstance(b, int) and b == 0 and g < 2):
                    pool.wait_ge(pv_done, b * STEPS + (g - 1) * NK)
                    pool.sem_inc(pool_past, 1)
                for j in range(J):
                    last = pool.tensor_copy(vp[g % 2][:, :, VW * j:VW * j + D],
                                            vs[:, :, D * (J * g + j):D * (J * g + j + 1)])
                last.then_inc(v_packed, 1)

            def residual(b):
                pool.wait_ge(xres_loaded, b * 16 + 16)
                pool.sem_inc(pool_past, 1)
                for qt in range(QT):
                    last = pool.tensor_tensor(xres[:, qt, :], xres[:, qt, :], bo[:], ALU.add)
                last.then_inc(xb_ready, 1)

            def gate_exponential(b):
                pool.wait_ge(gate_step, b * GATE_STEPS + 12)
                pool.sem_inc(pool_past, 1)
                pool.tensor_tensor(top[:, 5:6], euler[:], top[:, 4:5], ALU.pow).then_inc(gate_exp, 1)

            def scale_u(b):
                pool.wait_ge(gate_step, b * GATE_STEPS + 19)
                pool.sem_inc(pool_past, 1)
                for i in range(4):
                    last = pool.tensor_scalar(uc[:, i, :], uT[:, i, :], coef[:, i:i + 1], None, ALU.mult)
                last.then_inc(uc_ready, 1)

            def keep_wo(b, number):
                pool.wait_ge(ring_free, number + 1)
                pool.sem_inc(pool_past, 1)
                pool.tensor_copy(wT["o"][:], wall[:, 3]).then_inc(wo_kept, 1)

            pro = lambda job: st.loc_pro[job]
            layernorm(0)
            if not cross:
                gate_exponential(0)
                scale_u(0)
            split_q(0, pro)
            for c in range(NC):
                split_k(0, c, pro)
            pack_v(0, 0, pro)

            def body(b):
                post, prep = flags(b)
                here = lambda job: st.at(b, job)
                if post:
                    residual(b - 1)
                if prep:
                    layernorm(b + 1)
                pack_v(b, 1, None)
                if not cross:
                    keep_wo(b, st.at(b, ("O",)) if post else st.loc_pro[("W", 1)])
                    if prep:
                        gate_exponential(b + 1)
                        scale_u(b + 1)
                pack_v(b, 2, None)
                if prep:
                    split_q(b + 1, here)
                    if cross:
                        split_k(b + 1, 0, here)
                        split_k(b + 1, 1, here)
                        pack_v(b, 3, None)
                        split_k(b + 1, 2, here)
                        split_k(b + 1, 3, here)
                    else:
                        split_k(b + 1, 0, here)
                        pack_v(b, 3, None)
                    pack_v(b + 1, 0, here)
                else:
                    pack_v(b, 3, None)

            over_batches(pool, body)
            residual(B - 1)



def flamingo_layer(nc, x, ctxT, wx, we, y, out):
    with ExitStack() as sems:
        run_stage(nc, Stage(True), sems, x, y, ctxT, wx, "cross")
        run_stage(nc, Stage(False), sems, y, out, None, we, "expert")


def kernel(**inputs):
    import numpy as np
    import concourse.bacc as bacc
    from concourse.bass_utils import run_bass_kernel_spmd

    a = {n: np.asarray(v) for n, v in inputs.items()}

    def rows(v, n=128):
        return np.broadcast_to(v.reshape(1, -1), (n, v.size))

    def column(v):
        return v.reshape(-1, 128).T

    def paired(v):
        shape = v.shape[:-1]
        v = v.reshape(*shape, 2 * G, 2, D)
        return np.moveaxis(v, -2, -3).reshape(*shape, C)

    f, c = "L0_ffn_", "L0_xattn_"
    names = ("q", "k", "v", "o")
    data = {"x": a["x"], "ctxT": a["ctx_1024"].transpose(0, 2, 1)}
    wx = {"w" + n: a[c + "W" + n].T for n in names}
    wx |= {"bv": rows(a[c + "bv"]), "bo": rows(a[c + "bo"]),
           "gate": rows(a["g_xattn"])}
    we = {"w" + n: a[f + n + "Wm"].T for n in names}
    for d, bq, bk in ((wx, a[c + "bq"], a[c + "bk"]), (we, a[f + "qb"], a[f + "kb"])):
        d |= {"wq": paired(d["wq"]), "wk": paired(d["wk"]), "bq": column(paired(bq)), "bk": column(paired(bk))}
    we |= {"u": np.stack([(paired if n in "qk" else np.asarray)(a[f + n + "U"].transpose(0, 2, 1).reshape(EX * RANK, C))
                          for n in names]),
           "v": np.stack([a[f + n + "V"].reshape(EX * RANK, C) for n in names]),
           "s": np.stack([a[f + n + "S"].reshape(EX * RANK) for n in names], 1),
           "bv": rows(a[f + "vb"]), "bo": rows(a[f + "ob"]),
           "gate": rows(a["g_ffn"]), "gw1": a[f + "gw1"].T, "gw2": a[f + "gw2"].T,
           "gb1": a[f + "gb1"].reshape(-1, 1), "gb2": a[f + "gb2"].reshape(1, -1)}
    data |= {"x_" + n: v for n, v in wx.items()} | {"e_" + n: v for n, v in we.items()}

    nc = bacc.Bacc("TRN2", target_bir_lowering=False, num_devices=1)
    arrays, aps = {}, {}
    for name, v in data.items():
        arrays[f"in_{name}"] = np.ascontiguousarray(v)
        aps[name] = nc.dram_tensor(f"in_{name}", v.shape, mybir.dt.from_np(v.dtype), kind="ExternalInput").ap()
    y = nc.dram_tensor("after_cross", (B, T, C), F32, kind="Internal").ap()
    out = nc.dram_tensor("out", (B, T, C), F32, kind="ExternalOutput").ap()
    flamingo_layer(nc, aps["x"], aps["ctxT"], {n: aps["x_" + n] for n in wx}, {n: aps["e_" + n] for n in we}, y, out)
    r = run_bass_kernel_spmd(nc, [arrays], core_ids=[0])
    return r.results[0]["out"]
```

```python
from contextlib import ExitStack

import concourse.bass as bass
from concourse import mybir

F32 = mybir.dt.float32
BF16 = mybir.dt.bfloat16
ALU = mybir.AluOpType
ACT = mybir.ActivationFunctionType
AX = mybir.AxisListType

B, T, C = 16, 512, 256
KEYS = 1601
H, D = 16, 16
G, J = 4, 4
QT = T // 128
CC = C // 128
EX, RANK, GH = 8, 16, 64
VW = D + 1
VPAD = J * VW + 32 - VW
EPS = 1e-5
QSCALE = float(D) ** -0.5
TERMS = [(0, 0), (0, 1), (1, 0), (1, 1), (0, 2), (2, 0)]
MROW = [96, 32]
KROWS = [99, 128]
FILL_DMAS = 6
TAIL_JOBS = [("OT", G - 1), ("O", 0), ("O", 1)]
TAIL_TILES = [("aT", 0), ("aT", 1)]
NPROB = 4


def batch_of(b, job):
    if job[0] in ("aT", "O") or job == ("OT", G - 1):
        return b - 1
    if job[0] in ("OT", "S") or (job[0] in ("max", "M", "MS") and job[1] > 0):
        return b
    return b + 1


class Ring:

    def __init__(self, depth, prologue, plans, members, tail):
        pick = lambda ops: {op: n for n, op in enumerate(op for op in ops if op[0] in members)}
        self.depth = depth
        self.loc = {kind: pick(ops) for kind, ops in plans.items()}
        self.loc["prologue"] = pick(prologue)
        self.loc["tail"] = {op: n for n, op in enumerate(tail)}
        self.n_pro = len(self.loc["prologue"])
        self.per_iter = len(self.loc["mid"])
        assert self.per_iter % depth == 0

    def base(self, b):
        if isinstance(b, int) and b == 0:
            return self.n_pro
        return b * self.per_iter + (self.n_pro + len(self.loc["first"]) - self.per_iter)

    def end(self):
        return self.base(B - 1) + len(self.loc["last"])

    def context(self, b):
        if isinstance(b, str):
            return (0 if b == "prologue" else self.end()), self.loc[b]
        return self.base(b), self.loc[kind_of(b)]

    def at(self, b, op):
        base, loc = self.context(b)
        return base + loc[op]

    def slot(self, b, op):
        base, loc = self.context(1 if not isinstance(b, (int, str)) else b)
        return (base + loc[op]) % self.depth

    def before(self, b, op):
        if isinstance(b, int) and b == 0:
            return self.loc["prologue"][op]
        return self.base(b) + (self.loc["mid"][op] - self.per_iter)


def kind_of(b):
    if isinstance(b, int):
        return {0: "first", B - 1: "last"}.get(b, "mid")
    return "mid"


class Stage:

    def __init__(self, cross):
        self.cross = cross
        self.keys = KEYS if cross else T
        self.nk = -(-self.keys // 128)
        self.kr = [min(128, self.keys - 128 * k) for k in range(self.nk)]
        self.nc = -(-self.keys // 512)
        self.cw = [min(512, self.keys - 512 * c) for c in range(self.nc)]
        self.k_tiles = [("K", c, m) for c in range(self.nc) for m in ((0, 1) if self.cw[c] > 256 else (2,))]
        self.v_jobs = [(0, 2), (2, 4), (4, 6), (6, 8), (8, 10), (10, 11), (11, 12), (12, 13)] if cross else [(0, 4)]
        self.splits = 4 + 4 * self.nc
        q, v = [("Q", 0), ("Q", 1)], [("V", i) for i in range(len(self.v_jobs))]
        xt = [("xT", 0), ("xT", 1)]
        gates = [] if cross else [("h",), ("lg",), ("gb",), ("coef",)] + [("W", i) for i in range(4)]
        self.prologue = xt + gates + q + self.k_tiles + v + self.maxima(0) + [("MS", 0), ("M", 0)]
        plans = {"first": self.iteration(False, True), "mid": self.iteration(True, True),
                 "last": self.iteration(True, False)}
        self.plans = plans
        self.tiles = Ring(3, self.prologue, plans, ("S", "M", "xT", "aT", "Q", "K", "h", "gb"), TAIL_TILES)
        self.jobs = Ring(2, self.prologue, plans, ("max", "OT", "O", "V", "lg", "W"), TAIL_JOBS)

    def maxima(self, g):
        return [("max", g, hp, qt, c) for hp in range(2) for qt in range(QT) for c in range(self.nc)]

    def iteration(self, post, prep):
        k = self.k_tiles
        if self.cross:
            extra = [
                [(4, ("xT", 0)), (5, ("xT", 1)), (9, ("OT", 3)), (13, ("aT", 0)), (14, ("aT", 1)), (19, ("Q", 0)),
                 (25, ("O", 0)), (31, ("Q", 1)), (37, ("O", 1))],
                [(3, k[0]), (9, ("OT", 0)), (12, k[1]), (20, k[2]), (28, k[3]), (36, k[4])],
                [(0, k[5]), (6, k[6]), (9, ("OT", 1)), (15, ("V", 0)), (23, ("V", 1)), (31, ("V", 2)), (39, ("V", 3)),
                 (49, ("stats",))],
                [(9, ("OT", 2)), (12, ("V", 4)), (20, ("V", 5)), (27, ("V", 6)), (34, ("V", 7))],
            ]
            first, final, m_at = 0, 42, 48
        else:
            extra = [
                [(0, ("xT", 0)), (1, ("xT", 1)), (5, ("OT", 3)), (4, ("h",)), (7, ("aT", 0)), (7, ("aT", 1)),
                 (6, ("lg",)), (9, ("O", 0)), (10, ("O", 1)), (12, ("gb",)), (14, ("coef",))],
                [(3, ("W", 0)), (4, ("W", 1)), (5, ("OT", 0)), (6, ("Q", 0)), (8, ("Q", 1)), (9, k[0]), (11, k[1])],
                [(5, ("OT", 1)), (2, ("W", 2)), (3, ("W", 3)), (8, ("V", 0)), (11, ("stats",))],
                [(5, ("OT", 2))],
            ]
            first, final, m_at = 0, 10, 14
        out = []
        n = self.nk * J
        for g in range(G):
            mx = self.maxima((g + 1) % G) if g < G - 1 or prep else []
            lo = first if self.cross or g < G - 1 else 3
            here = [[] for _ in range(n)]
            for i, job in enumerate(mx):
                here[lo + i * (final - lo) // len(mx)].append(job)
            if mx:
                here[final].append(("MS", (g + 1) % G))
                here[m_at].append(("M", (g + 1) % G))
            for at, op in extra[g]:
                of_last = op[0] in ("aT", "O") or op == ("OT", G - 1)
                if (post if of_last else op[0] == "OT" or prep):
                    here[at].insert(0 if op[0] == "OT" else len(here[at]), op)
            i = 0
            for kt in range(self.nk):
                for j in range(J):
                    out += here[i] + [("S", g, kt, j)]
                    i += 1
                if g or kt or post:
                    out.append(("PV", (g * self.nk + kt - 1) % (G * self.nk)))
                if kt == 0 and (g or post):
                    out.append(("HC", (g - 1) % G))
        return out


def run_stage(nc, st, sems, x_in, x_out, ctxT, w, stacks, tag):
    cross, NK, NC, KR, CW = st.cross, st.nk, st.nc, st.kr, st.cw
    tiles, jobs = st.tiles, st.jobs
    NT = J * NK
    STEPS = G * NK
    LAST_V = ("V", len(st.v_jobs) - 1)
    LAST_K = {c: [k for k in st.k_tiles if k[1] == c][-1] for c in range(NC)}
    ctx = ExitStack()
    with ctx:
        def sb(name, shape, dt=F32):
            return ctx.enter_context(nc.sbuf_tensor(f"{tag}_{name}", shape, dt))

        def sem(name):
            return sems.enter_context(nc.semaphore(f"{tag}_{name}"))

        ring = [ctx.enter_context(nc.psum_tensor(f"{tag}_ring{i}", [128, 2, 512], F32)) for i in range(2)]
        tile = [ctx.enter_context(nc.psum_tensor(f"{tag}_tile{i}", [128, 512], F32)) for i in range(3)]
        heads = ctx.enter_context(nc.psum_tensor(f"{tag}_heads", [128, 512], F32))

        xt = sb("xt", [128, QT, C])
        xT = sb("xT", [128, CC, T])
        xres = sb("xres", [128, QT, C])
        xo = sb("xo", [128, QT, C])
        qf = sb("qf", [128, CC, T])
        kf = [sb(f"kf{i}", [128, CC, 512]) for i in range(2)]
        rest = sb("rest", [128, CC, 512])
        parts = [sb(f"parts{i}", [128, 3, CC, 512], BF16) for i in range(2)]
        kst = sb("kst", [128, G, J, st.keys], BF16)
        qst = sb("qst", [128, G, J, T], BF16)
        vs = sb("vs", [128, NK, C])
        vp = [sb(f"vp{i}", [128, NK, VPAD]) for i in range(2)]
        prob = [sb(f"prob{i}", [128, J, T]) for i in range(NPROB)]
        hsb = sb("hsb", [128, T])
        attn = sb("attn", [128, QT, C])
        attnT = sb("attnT", [128, CC, T])
        rden = sb("rden", [128, QT, J])
        stats = sb("stats", [128, QT, 6])
        mv = sb("mv", [128, QT, 2])
        veps = sb("veps", [128, QT])
        nmean = sb("nmean", [128, QT])
        rstd = sb("rstd", [128, QT])
        nhalf = sb("nhalf", [128, QT])
        mxp = sb("mxp", [128, 2 * QT, 2, NC])
        negm = sb("negm", [128, 2 * QT, 2])
        mrest = sb("mrest", [128, 2 * QT, 2])
        mparts = sb("mparts", [128, 2 * QT, 128], BF16)
        ident = sb("ident", [128, 128])
        identb = sb("identb", [128, 128], BF16)
        bq = sb("bq", [128, CC])
        bk = sb("bk", [128, CC])
        bv = sb("bv", [128, C])
        bo = sb("bo", [128, C])
        gate = sb("gate", [128, 1])
        weights = ["q", "k", "v", "o"]
        if cross:
            cT = sb("cT", [128, CC, KEYS])
            wT = {n: sb(f"w{n}", [128, CC, C]) for n in weights}
        else:
            cT = xT
            wall = sb("wall", [128, 4, CC, C])
            wT = {n: wall[:, i] for i, n in enumerate(weights)}
            wT["o"] = sb("wo_now", [128, CC, C])
            wm = sb("wm", [128, 4, CC, C])
            uT = sb("uT", [128, 4, C])
            vw = sb("vw", [128, 4, C])
            uc = sb("uc", [128, 4, C])
            sv = sb("sv", [128, 4])
            coef = sb("coef", [128, 4])
            gw1 = sb("gw1", [128, CC, GH])
            gw2 = sb("gw2", [GH, EX])
            gb1 = sb("gb1", [GH, 1])
            gb2 = sb("gb2", [1, EX])
            prio = sb("prio", [1, EX])
            onehot = sb("onehot", [128, EX])
            ones = sb("ones", [1, 128])
            euler = sb("euler", [1, 1])
            pooled = sb("pooled", [128, CC])
            hid = sb("hid", [GH, 1])
            lg = sb("lg", [1, EX])
            lg2 = sb("lg2", [1, EX])
            top = sb("top", [1, 8])
            cand = sb("cand", [1, 2, EX])
            pick = sb("pick", [1, 2, EX])
            gates = sb("gates", [1, 2, EX])
            gsel = sb("gsel", [128, EX])
            gsb = sb("gsb", [128, EX])
            csum = sb("csum", [128, 1])

        pool_past, sp_past, dve_past, pe_past = (sem(f"{e}_past") for e in ("pool", "sp", "dve", "pe"))
        w_loaded = sem("w_loaded")
        const_dve = sem("const_dve")
        const_pool = sem("const_pool")
        gate_tanh = sem("gate_tanh")
        x_loaded = sem("x_loaded")
        ctx_loaded = sem("ctx_loaded")
        xres_loaded = sem("xres_loaded")
        fill_done = [sem(f"fill_done{g}") for g in range(G)]
        parts_out = [sem(f"parts_out{i}") for i in range(2)]
        stored = sem("stored")
        ring_full = sem("ring_full")
        ring_free = sem("ring_free")
        tile_full = sem("tile_full")
        tile_done = sem("tile_done")
        pv_done = sem("pv_done")
        heads_copied = sem("heads_copied")
        stats_done = sem("stats_done")
        stats_step = sem("stats_step")
        ln_step = sem("ln_step")
        xhat_ready = sem("xhat_ready")
        xb_ready = sem("xb_ready")
        split = sem("split")
        v_packed = sem("v_packed")
        m_step = sem("m_step")
        den_ready = sem("den_ready")
        if not cross:
            gate_step = sem("gate_step")
            gate_exp = sem("gate_exp")
            uc_ready = sem("uc_ready")
            wo_kept = sem("wo_kept")
        GATE_STEPS = 18
        CONST_DVE, CONST_POOL = (8, 7) if cross else (9, 12 + EX)
        block = ctx.enter_context(nc.Block())

        x_rows = x_in.rearrange("b (p t) c -> b p t c", t=QT)
        out_rows = x_out.rearrange("b (p t) c -> b p t c", t=QT)
        n_weights = 9 if cross else 16

        def over_batches(engine, body):
            body(0)
            with engine.Fori(1, B - 2) as b:
                body(b)
            body(B - 2)
            body(B - 1)

        def flags(b):
            known = isinstance(b, int)
            return not (known and b == 0), not (known and b == B - 1), not (known and b >= B - 2)

        def parts_written(c):
            buffer = (c + 1) % 2
            here = len([x for x in range(-1, c + 1) if (x + 1) % 2 == buffer])
            per_batch = len([x for x in range(-1, NC) if (x + 1) % 2 == buffer])
            return buffer, here * len(TERMS) * 16, per_batch * len(TERMS) * 16

        @block.sync
        def _(sp):
            loads = []
            if cross:
                loads += [(wT[n][:], w["w" + n].rearrange("(c p) o -> p c o", p=128)) for n in weights]
                loads += [(bo[:], w["bo"]), (bv[:], w["bv"]), (bq[:], w["bq"]), (bk[:], w["bk"]), (gate[:], w["gate"])]
            else:
                loads += [(wm[:, i], w["w" + n].rearrange("(c p) o -> p c o", p=128)) for i, n in enumerate(weights)]
                loads += [(uT[:], w["u"].rearrange("n p o -> p n o")), (vw[:], w["v"].rearrange("n p o -> p n o")),
                          (sv[:], w["s"]), (bo[:], w["bo"]), (bv[:], w["bv"]), (bq[:], w["bq"]), (bk[:], w["bk"]),
                          (gate[:], w["gate"]), (gw1[:], w["gw1"].rearrange("(c p) o -> p c o", p=128)),
                          (gw2[:], w["gw2"]), (gb1[:], w["gb1"]), (gb2[:], w["gb2"])]
            assert len(loads) == n_weights
            sp.dma_start(xt[:], x_rows[0]).then_inc(x_loaded, 16)
            if cross:
                sp.dma_start(cT[:], ctxT[0].rearrange("(c p) k -> p c k", p=128)).then_inc(ctx_loaded, 16)
            for dst, src in loads:
                sp.dma_start(dst, src).then_inc(w_loaded, 16)

            qd, kd = stacks

            def write_parts(b, c):
                buffer = (c + 1) % 2
                width = T if c < 0 else CW[c]
                cols = slice(0, T) if c < 0 else slice(512 * c, 512 * c + CW[c])
                sp.wait_ge(split, b * st.splits + 4 * (c + 2))
                sp.sem_inc(sp_past, 1)
                for s, term in enumerate(TERMS):
                    if c < 0:
                        sp.dma_start(qd[:, s, :, :, cols], parts[buffer][:, term[0], :, 0:width])\
                            .then_inc(parts_out[buffer], 16)
                    else:
                        sp.dma_start(kd[:, s, :, :, cols], parts[buffer][:, term[1], :, 0:width])\
                            .then_inc(parts_out[buffer], 16)

            def parts_in_dram(b):
                for c in (NC - 2, NC - 1):
                    buffer, here, per_batch = parts_written(c)
                    sp.wait_ge(parts_out[buffer], b * per_batch + here)
                    sp.sem_inc(sp_past, 1)

            def stacks_read(b):
                for g in range(G):
                    sp.wait_ge(fill_done[g], b * (FILL_DMAS * 16))
                    sp.sem_inc(sp_past, 1)

            def fill(b, g):
                if not (isinstance(b, int) and b == 0):
                    sp.wait_ge(tile_full, last_score(b, g) + 1)
                for stack, src in ((qst, qd), (kst, kd)):
                    sp.dma_start(stack[0:96, g, 0:2, :], src[2 * g].rearrange("s d h n -> (s d) h n"))\
                        .then_inc(fill_done[g], 16)
                    sp.dma_start(stack[64:128, g, 2:4, :], src[2 * g + 1, 0:4].rearrange("s d h n -> (s d) h n"))\
                        .then_inc(fill_done[g], 16)
                    sp.dma_start(stack[0:32, g, 2:4, :], src[2 * g + 1, 4:6].rearrange("s d h n -> (s d) h n"))\
                        .then_inc(fill_done[g], 16)

            def last_score(b, g):
                if isinstance(b, int) and b == 1:
                    return tiles.at(0, ("S", g, NK - 1, J - 1))
                return tiles.base(b) + (tiles.loc["mid"][("S", g, NK - 1, J - 1)] - tiles.per_iter)

            sp.wait_ge(const_pool, CONST_POOL)
            sp.wait_ge(tile_done, tiles.at("prologue", ("xT", 1)) + 1)
            sp.dma_start(xt[:], x_rows[1]).then_inc(x_loaded, 16)
            for c in range(-1, NC):
                write_parts(0, c)
            parts_in_dram(0)
            for g in range(3):
                fill(0, g)

            def body(b):
                post, prep, ahead = flags(b)
                if post:
                    if not isinstance(b, int) or b > 1:
                        sp.wait_ge(ring_free, jobs.before(b, ("O", 1)) + 1)
                        sp.sem_inc(sp_past, 1)
                    sp.dma_start(xres[:], x_rows[b - 1]).then_inc(xres_loaded, 16)
                if prep and cross:
                    sp.wait_ge(ring_free, jobs.before(b, LAST_V) + 1)
                    sp.sem_inc(sp_past, 1)
                    sp.dma_start(cT[:], ctxT[b + 1].rearrange("(c p) k -> p c k", p=128)).then_inc(ctx_loaded, 16)
                fill(b, 3)
                if ahead:
                    sp.wait_ge(tile_done, tiles.at(b, ("xT", 1)) + 1)
                    sp.sem_inc(sp_past, 1)
                    sp.dma_start(xt[:], x_rows[b + 2]).then_inc(x_loaded, 16)
                if prep:
                    stacks_read(b + 1)
                    if cross:
                        write_parts(b + 1, -1)
                if post:
                    sp.wait_ge(ring_free, jobs.at(b, ("O", 1)) + 1)
                    sp.sem_inc(sp_past, 1)
                    sp.dma_start(out_rows[b - 1], xo[:]).then_inc(stored, 16)
                if prep:
                    for c in range(0 if cross else -1, NC):
                        write_parts(b + 1, c)
                    parts_in_dram(b + 1)
                    for g in range(3):
                        fill(b + 1, g)

            over_batches(sp, body)
            sp.wait_ge(ring_free, jobs.at(B - 1, ("O", 1)) + 1)
            sp.dma_start(xres[:], x_rows[B - 1]).then_inc(xres_loaded, 16)
            sp.wait_ge(ring_free, jobs.at("tail", ("O", 1)) + 1)
            sp.dma_start(out_rows[B - 1], xo[:]).then_inc(stored, 16)
            sp.wait_ge(stored, 16 * B)

        @block.tensor
        def _(pe):
            def slot_free(where, ring, op, done, after=None):
                base, loc = ring.context(where)
                least = max(loc[op] - ring.depth + 1, loc[after] + 1 if after else -10 ** 9)
                if not isinstance(base, int) or base + least > 0:
                    pe.wait_ge(done, base + least)

            def job(where, b, op):
                slot, kind = ring[jobs.slot(where, op)], op[0]
                slot_free(where, jobs, op, ring_free, ("W", 2) if kind == "V" and not cross else None)
                if kind == "max":
                    _, g, hp, qt, c = op
                    pe.wait_ge(fill_done[g], b * (FILL_DMAS * 16) + FILL_DMAS * 16)
                    for e in range(2):
                        j, r = 2 * e + hp, 64 * e
                        mm = pe.matmul(slot[:, 1 - e, 0:CW[c]], qst[r:r + 64, g, j, 128 * qt:128 * qt + 128],
                                       kst[r:r + 64, g, j, 512 * c:512 * c + CW[c]], start=True, stop=True)
                elif kind == "OT":
                    pe.wait_ge(heads_copied, b * G + op[1] + 1)
                    for qt in range(QT):
                        mm = pe.transpose(slot[:, 0, 128 * qt:128 * qt + 128], hsb[:, 128 * qt:128 * qt + 128], ident[:])
                elif kind == "O":
                    pe.wait_ge(tile_done, tiles.at(where, ("aT", 1)) + 1)
                    if not cross:
                        pe.wait_ge(wo_kept, b + 1)
                    for i in range(2):
                        qt = 2 * op[1] + i
                        for c in range(CC):
                            mm = pe.matmul(slot[:, 0, 256 * i:256 * i + 256], attnT[:, c, 128 * qt:128 * qt + 128],
                                           wT["o"][:, c, :], start=(c == 0), stop=(c == CC - 1))
                elif kind == "V":
                    k0, k1 = st.v_jobs[op[1]]
                    if cross:
                        pe.wait_ge(ctx_loaded, b * 16 + 16)
                    for i, kt in enumerate(range(k0, k1)):
                        for c in range(CC):
                            mm = pe.matmul(slot[0:KR[kt], i // 2, 256 * (i % 2):256 * (i % 2) + 256],
                                           cT[:, c, 128 * kt:128 * kt + KR[kt]], wT["v"][:, c, :],
                                           start=(c == 0), stop=(c == CC - 1))
                elif kind == "lg":
                    pe.wait_ge(tile_done, tiles.at(where, ("h",)) + 1)
                    pe.sem_inc(pe_past, 1)
                    mm = pe.matmul(slot[0:1, 0, 0:EX], hid[:], gw2[:], start=True, stop=True)
                elif kind == "W":
                    pe.wait_ge(uc_ready, b + 1)
                    for c in range(CC):
                        mm = pe.matmul(slot[:, 0, 256 * c:256 * c + 256], vw[:, op[1], 128 * c:128 * c + 128],
                                       uc[:, op[1], :], start=True, stop=True)
                mm.then_inc(ring_full, 1)

            def tile_use(where, b, op):
                n, kind = tiles.slot(where, op), op[0]
                bank = tile[n]
                slot_free(where, tiles, op, tile_done, {"Q": ("xT", 1), "h": ("xT", 1)}.get(kind))
                if kind == "S":
                    _, g, kt, j = op
                    if isinstance(b, int) and (b, g, kt) == (0, 0, 0):
                        pe.wait_ge(tile_done, tiles.at("prologue", ("M", 0)) + 1)
                    rows = KROWS[j // 2]
                    mm = pe.matmul(bank[0:KR[kt], :], kst[0:rows, g, j, 128 * kt:128 * kt + KR[kt]],
                                   qst[0:rows, g, j, :], start=True, stop=True)
                elif kind == "M":
                    pe.wait_ge(m_step, b * (5 * G) + 5 * (op[1] + 1))
                    for i in range(2 * QT):
                        mm = pe.transpose(bank[:, 64 * i:64 * i + 64].bitcast(BF16), mparts[:, i, :], identb[:])
                elif kind in ("xT", "aT"):
                    if kind == "xT":
                        pe.wait_ge(xhat_ready, b + 1)
                    else:
                        pe.wait_ge(ring_free, jobs.at(where, ("OT", G - 1)) + 1)
                    src, c = (xt if kind == "xT" else attn), op[1]
                    for qt in range(QT):
                        mm = pe.transpose(bank[:, 128 * qt:128 * qt + 128], src[:, qt, 128 * c:128 * c + 128], ident[:])
                elif kind == "Q":
                    if not cross:
                        pe.wait_ge(ring_free, jobs.at(where, ("W", 0)) + 1)
                    m = op[1]
                    for c in range(CC):
                        mm = pe.matmul(bank[:, :], wT["q"][:, c, 128 * m:128 * m + 128], xT[:, c, :],
                                       start=(c == 0), stop=(c == CC - 1))
                elif kind == "K":
                    _, k, which = op
                    if cross:
                        pe.wait_ge(ctx_loaded, b * 16 + 16)
                    else:
                        pe.wait_ge(ring_free, jobs.at(where, ("W", 1)) + 1)
                    for m in ((0, 1) if which == 2 else (which,)):
                        out = bank[:, CW[k] * m:CW[k] * (m + 1)] if which == 2 else bank[:, 0:CW[k]]
                        for c in range(CC):
                            mm = pe.matmul(out, wT["k"][:, c, 128 * m:128 * m + 128],
                                           cT[:, c, 512 * k:512 * k + CW[k]], start=(c == 0), stop=(c == CC - 1))
                elif kind == "h":
                    for c in range(CC):
                        mm = pe.matmul(bank[0:GH, 0:1], gw1[:, c, :], pooled[:, c:c + 1],
                                       start=(c == 0), stop=(c == CC - 1))
                elif kind == "gb":
                    pe.wait_ge(gate_step, b * GATE_STEPS + 15)
                    mm = pe.matmul(bank[:, 0:EX], ones[:], gates[:, 1, :], start=True, stop=True)
                mm.then_inc(tile_full, 1)

            def pv_step(b, s, exps):
                g, kt = divmod(s, NK)
                pe.wait_ge(tile_done, exps + 1)
                if kt == 0:
                    pe.wait_ge(v_packed, b * G + g + 1)
                    if not (isinstance(b, int) and b == 0 and g == 0):
                        pe.wait_ge(heads_copied, b * G + g)
                for j in range(J):
                    mm = pe.matmul(heads[32 * j:32 * j + 32, :], vp[g % 2][0:KR[kt], kt, VW * j:VW * j + 32],
                                   prob[s % NPROB][0:KR[kt], j, :], start=(kt == 0), stop=(kt == NK - 1))
                mm.then_inc(pv_done, 1)

            pe.wait_ge(w_loaded, 16 * n_weights)
            pe.wait_ge(const_dve, CONST_DVE)
            pe.wait_ge(const_pool, CONST_POOL)

            def one(where, b, op):
                if op in jobs.context(where)[1]:
                    job(where, b, op)
                elif op in tiles.context(where)[1]:
                    tile_use(where, b, op)

            for op in st.prologue:
                one("prologue", 0, op)

            def body(b):
                for op in st.plans[kind_of(b)]:
                    if op[0] != "PV":
                        one(b, batch_of(b, op), op)
                    elif op[1] < STEPS - 1:
                        pv_step(b, op[1], tiles.at(b, ("S", *divmod(op[1], NK), J - 1)))
                    else:
                        pv_step(b - 1, STEPS - 1, tiles.base(b) - 1)

            over_batches(pe, body)
            pv_step(B - 1, STEPS - 1, tiles.end() - 1)
            for op in (TAIL_JOBS[0], *TAIL_TILES, *TAIL_JOBS[1:]):
                one("tail", B - 1, op)

        @block.scalar
        def _(act):
            act.wait_ge(w_loaded, 16 * n_weights)
            act.activation(gate[:], gate[:], ACT.Tanh).then_inc(gate_tanh, 1)
            act.wait_ge(const_dve, CONST_DVE)
            act.wait_ge(const_pool, CONST_POOL)

            def tile_use(where, b, op):
                bank, kind = tile[tiles.slot(where, op)], op[0]
                if kind == "S":
                    _, g, kt, j = op
                    s = g * NK + kt
                    if j == 0 and not (isinstance(b, int) and b == 0 and s < NPROB):
                        act.wait_ge(pv_done, b * STEPS + s - NPROB + 1)
                    act.wait_ge(tile_full, tiles.at(where, op) + 1)
                    done = act.activation(prob[s % NPROB][0:KR[kt], j, :], bank[0:KR[kt], :], ACT.Exp)
                    done.then_inc(tile_done, 1)
                    return
                if kind == "Q" or kind == "K":
                    c = op[1]
                    if kind == "K" and c >= 2:
                        act.wait_ge(split, b * st.splits + 4 + 4 * (c - 2) + 2)
                    elif not (isinstance(b, int) and b == 0):
                        act.wait_ge(split, b * st.splits)
                act.wait_ge(tile_full, tiles.at(where, op) + 1)
                if kind == "M":
                    g = op[1]
                    seen = bank[:, :].bitcast(BF16).rearrange("p (h q) -> p h q", h=2)
                    act.activation(qst[32:64, g, 2:4, :], seen[32:64], ACT.Copy)
                    done = act.activation(qst[96:99, g, 0:2, :], seen[96:99], ACT.Copy)
                elif kind == "aT":
                    done = act.activation(attnT[:, op[1], :], bank[:, :], ACT.Copy)
                elif kind == "xT" and cross:
                    done = act.activation(xT[:, op[1], :], bank[:, :], ACT.Copy)
                elif kind == "xT":
                    done = act.activation(xT[:, op[1], :], bank[:, :], ACT.Copy, accum_out=pooled[:, op[1]:op[1] + 1])
                elif kind == "Q":
                    m = op[1]
                    done = act.activation(qf[:, m, :], bank[:, :], ACT.Identity, bias=bq[:, m:m + 1], scale=QSCALE)
                elif kind == "K":
                    _, c, which = op
                    for m in ((0, 1) if which == 2 else (which,)):
                        src = bank[:, CW[c] * m:CW[c] * (m + 1)] if which == 2 else bank[:, 0:CW[c]]
                        done = act.activation(kf[c % 2][:, m, 0:CW[c]], src, ACT.Identity, bias=bk[:, m:m + 1])
                elif kind == "h":
                    done = act.activation(hid[:], bank[0:GH, 0:1], ACT.Relu, bias=gb1[:], scale=1.0 / T)
                elif kind == "gb":
                    done = act.activation(gsb[:], bank[:, 0:EX], ACT.Copy)
                done.then_inc(tile_done, 1)

            def copy_heads(b, g, last_ot):
                act.wait_ge(pv_done, b * STEPS + (g + 1) * NK)
                if last_ot is not None:
                    act.wait_ge(ring_full, last_ot + 1)
                act.activation(hsb[:], heads[:], ACT.Copy).then_inc(heads_copied, 1)

            for op in st.prologue:
                if op in tiles.loc["prologue"]:
                    tile_use("prologue", 0, op)

            def body(b):
                post, _, _ = flags(b)
                for op in st.plans[kind_of(b)]:
                    if op in tiles.loc[kind_of(b)]:
                        tile_use(b, batch_of(b, op), op)
                    elif op == ("HC", G - 1):
                        copy_heads(b - 1, G - 1, jobs.before(b, ("OT", G - 2)))
                    elif op[0] == "HC":
                        g = op[1]
                        copy_heads(b, g, jobs.at(b, ("OT", (g - 1) % G)) if g or post else None)

            over_batches(act, body)
            copy_heads(B - 1, G - 1, jobs.at(B - 1, ("OT", G - 2)))
            for op in TAIL_TILES:
                tile_use("tail", B - 1, op)

        @block.vector
        def _(dve):
            dve.memset(vs[:], 0.0).then_inc(const_dve, 1)
            dve.memset(vp[0][:], 1.0).then_inc(const_dve, 1)
            dve.memset(vp[1][:], 1.0).then_inc(const_dve, 1)
            dve.memset(mparts[:], 0.0).then_inc(const_dve, 1)
            dve.wait_ge(const_pool, CONST_POOL)
            dve.tensor_copy(identb[:], ident[:]).then_inc(const_dve, 1)
            dve.wait_ge(w_loaded, 16 * n_weights)
            dve.tensor_scalar(bq[:], bq[:], QSCALE, None, ALU.mult).then_inc(const_dve, 1)
            dve.wait_ge(gate_tanh, 1)
            dve.tensor_scalar(bo[:], bo[:], gate[:], None, ALU.mult).then_inc(const_dve, 1)
            if cross:
                dve.tensor_scalar(wT["o"][:], wT["o"][:], gate[:], None, ALU.mult).then_inc(const_dve, 1)
            else:
                dve.tensor_scalar(wm[:, 3], wm[:, 3], gate[:], None, ALU.mult).then_inc(const_dve, 1)
                dve.tensor_scalar(sv[:, 3:4], sv[:, 3:4], gate[:], None, ALU.mult).then_inc(const_dve, 1)
            dve.wait_ge(const_dve, CONST_DVE)

            def layernorm_stats(b):
                dve.wait_ge(x_loaded, b * 16 + 16)
                if not isinstance(b, int) or b > 0:
                    dve.wait_ge(xhat_ready, b)
                for qt in range(QT):
                    last = dve.bn_stats(stats[:, qt, :], xt[:, qt, :])
                last.then_inc(stats_step, 1)
                dve.wait_ge(stats_step, b + 1)
                dve.sem_inc(dve_past, 1)
                for qt in range(QT):
                    last = dve.bn_aggr(mv[:, qt, :], stats[:, qt, :])
                last.then_inc(stats_done, 1)

            def job(where, b, op):
                slot, kind = ring[jobs.slot(where, op)], op[0]
                n = jobs.at(where, op)
                if kind == "OT":
                    dve.wait_ge(ring_free, n)
                if kind == "V" and op[1] == 0 and not (isinstance(b, int) and b == 0):
                    dve.wait_ge(v_packed, b * G)
                if kind == "O":
                    dve.wait_ge(xb_ready, b + 1)
                    if not (isinstance(b, int) and b == 0):
                        dve.wait_ge(stored, b * 16)
                if kind == "W" and op[1] == 3 and not (isinstance(b, int) and b == 0):
                    dve.wait_ge(wo_kept, b)
                dve.wait_ge(ring_full, n + 1)
                if kind == "max":
                    _, g, hp, qt, c = op
                    done = dve.tensor_reduce(mxp[:, QT * hp + qt, :, c], slot[:, :, 0:CW[c]], AX.X, ALU.max)
                elif kind == "OT":
                    g = op[1]
                    seen = slot[:, 0, :].rearrange("p (q j d) -> p q j d", q=QT, j=J)
                    dve.reciprocal(rden[:], seen[:, :, :, D]).then_inc(den_ready, 1)
                    dve.wait_ge(den_ready, b * G + g + 1)
                    done = dve.tensor_tensor(
                        attn[:, :, D * J * g:D * J * (g + 1)].rearrange("p q (j d) -> p q j d", j=J),
                        seen[:, :, :, 0:D], rden[:].unsqueeze(3).broadcast_to([128, QT, J, D]), ALU.mult)
                elif kind == "O":
                    i = 2 * op[1]
                    done = dve.tensor_tensor(xo[:, i:i + 2, :].rearrange("p q c -> p (q c)"),
                                             xres[:, i:i + 2, :].rearrange("p q c -> p (q c)"), slot[:, 0, :], ALU.add)
                elif kind == "V":
                    k0, k1 = st.v_jobs[op[1]]
                    kr = KR[k1 - 1]
                    done = dve.tensor_tensor(
                        vs[0:kr, k0:k1, :],
                        slot[0:kr].rearrange("p a (b n) -> p (a b) n", n=C)[:, 0:k1 - k0, :],
                        bv[0:kr].unsqueeze(1).broadcast_to([kr, k1 - k0, C]), ALU.add)
                elif kind == "lg":
                    done = dve.tensor_tensor(lg[:], gb2[:], slot[0:1, 0, 0:EX], ALU.add)
                elif kind == "W":
                    i = op[1]
                    done = dve.tensor_tensor(wall[:, i].rearrange("p c n -> p (c n)"),
                                             wm[:, i].rearrange("p c n -> p (c n)"), slot[:, 0, :], ALU.add)
                done.then_inc(ring_free, 1)
                if kind == "lg":
                    choose(b, n)

            def max_parts(b, g, maxima):
                k = b * (5 * G) + 5 * g
                at = lambda part: mparts[:, :, 32 + part:128:64]
                dve.wait_ge(ring_free, maxima + 1)
                dve.tensor_reduce(negm[:], mxp[:], AX.X, ALU.max, negate=True).then_inc(m_step, 1)
                dve.wait_ge(m_step, k + 1)
                dve.tensor_copy(at(0), negm[:]).then_inc(m_step, 1)
                dve.wait_ge(m_step, k + 2)
                dve.tensor_tensor(mrest[:], negm[:], at(0), ALU.subtract).then_inc(m_step, 1)
                dve.wait_ge(m_step, k + 3)
                dve.tensor_copy(at(1), mrest[:]).then_inc(m_step, 1)
                dve.wait_ge(m_step, k + 4)
                dve.tensor_tensor(at(2), mrest[:], at(1), ALU.subtract).then_inc(m_step, 1)
                dve.wait_ge(m_step, k + 5)

            def coefficients(b, gates_copied):
                k = b * GATE_STEPS + 15
                dve.wait_ge(tile_done, gates_copied + 1)
                dve.tensor_tensor(gsel[:], onehot[:], gsb[:], ALU.mult).then_inc(gate_step, 1)
                dve.wait_ge(gate_step, k + 1)
                dve.tensor_reduce(csum[:], gsel[:], AX.X, ALU.add).then_inc(gate_step, 1)
                dve.wait_ge(gate_step, k + 2)
                dve.tensor_scalar(coef[:], sv[:], csum[:], None, ALU.mult).then_inc(gate_step, 1)

            def choose(b, n):
                k = [b * GATE_STEPS]

                def done(op):
                    op.then_inc(gate_step, 1)
                    k[0] = k[0] + 1
                    dve.wait_ge(gate_step, k[0])

                dve.wait_ge(ring_free, n + 1)
                for r, row in ((0, lg), (1, lg2)):
                    if r:
                        done(dve.scalar_tensor_tensor(lg2[:], pick[:, 0, :], -3.0e38, lg[:], ALU.mult, ALU.add))
                    done(dve.tensor_reduce(top[:, 2 * r:2 * r + 1], row[:], AX.X, ALU.max))
                    done(dve.scalar_tensor_tensor(cand[:, r, :], row[:], top[:, 2 * r:2 * r + 1], prio[:],
                                                  ALU.is_ge, ALU.mult))
                    done(dve.tensor_reduce(top[:, 2 * r + 1:2 * r + 2], cand[:, r, :], AX.X, ALU.max))
                    done(dve.tensor_scalar(pick[:, r, :], cand[:, r, :], top[:, 2 * r + 1:2 * r + 2], None, ALU.is_equal))
                done(dve.tensor_tensor(top[:, 4:5], top[:, 2:3], top[:, 0:1], ALU.subtract))
                dve.wait_ge(gate_exp, b + 1)
                done(dve.tensor_scalar(top[:, 6:7], top[:, 5:6], 1.0, None, ALU.add))
                done(dve.reciprocal(top[:, 7:8], top[:, 6:7]))
                done(dve.tensor_scalar(gates[:, 0, :], pick[:, 1, :], top[:, 5:6], None, ALU.mult))
                done(dve.tensor_tensor(gates[:, 0, :], gates[:, 0, :], pick[:, 0, :], ALU.add))
                done(dve.tensor_scalar(gates[:, 1, :], gates[:, 0, :], top[:, 7:8], None, ALU.mult))

            layernorm_stats(0)

            def one(where, b, op):
                if op in jobs.context(where)[1]:
                    job(where, b, op)
                elif op[0] == "MS":
                    max_parts(b, op[1], jobs.at(where, ("max", op[1], 1, QT - 1, NC - 1)))
                elif op[0] == "coef":
                    coefficients(b, tiles.at(where, ("gb",)))

            for op in st.prologue:
                one("prologue", 0, op)
                if op == ("xT", 1):
                    layernorm_stats(1)

            def body(b):
                _, _, ahead = flags(b)
                for op in st.plans[kind_of(b)]:
                    if op[0] != "stats":
                        one(b, batch_of(b, op), op)
                    elif ahead:
                        layernorm_stats(b + 2)

            over_batches(dve, body)
            for op in TAIL_JOBS:
                one("tail", B - 1, op)

        @block.gpsimd
        def _(pool):
            pool.memset(ident[:], 0.0).then_inc(const_pool, 1)
            pool.wait_ge(const_pool, 1)
            pool.affine_select(out=ident[:], in_=ident[:], compare_op=ALU.not_equal, fill=1.0, base=0,
                               pattern=[[-1, 128]], channel_multiplier=1).then_inc(const_pool, 1)
            pool.wait_ge(const_pool, 2)
            pool.memset(kst[96:128, :, 0:2, :], 1.0).then_inc(const_pool, 1)
            pool.wait_ge(const_pool, 3)
            pool.memset(kst[32:64, :, 2:4, :], 0.0).then_inc(const_pool, 1)
            pool.wait_ge(const_pool, 4)
            pool.memset(qst[32:64, :, 2:4, :], 0.0).then_inc(const_pool, 1)
            pool.wait_ge(const_pool, 5)
            pool.memset(kst[32:35, :, 2:4, :], 1.0).then_inc(const_pool, 1)
            pool.wait_ge(const_pool, 6)
            pool.memset(nhalf[:], -0.5).then_inc(const_pool, 1)
            pool.wait_ge(const_pool, 7)
            if not cross:
                for e in range(EX):
                    pool.memset(prio[:, e:e + 1], float(EX - e)).then_inc(const_pool, 1)
                    pool.wait_ge(const_pool, 8 + e)
                pool.memset(ones[:], 1.0).then_inc(const_pool, 1)
                pool.wait_ge(const_pool, 8 + EX)
                pool.memset(euler[:], 2.718281828459045).then_inc(const_pool, 1)
                pool.wait_ge(const_pool, 9 + EX)
                pool.memset(onehot[:], 1.0).then_inc(const_pool, 1)
                pool.wait_ge(const_pool, 10 + EX)
                pool.affine_select(out=onehot[:], in_=onehot[:], compare_op=ALU.is_ge, fill=0.0, base=0,
                                   pattern=[[-RANK, EX]], channel_multiplier=1).then_inc(const_pool, 1)
                pool.wait_ge(const_pool, 11 + EX)
                pool.affine_select(out=onehot[:], in_=onehot[:], compare_op=ALU.is_ge, fill=0.0, base=RANK - 1,
                                   pattern=[[RANK, EX]], channel_multiplier=-1).then_inc(const_pool, 1)
            pool.wait_ge(const_pool, CONST_POOL)
            pool.wait_ge(const_dve, CONST_DVE)

            def layernorm(b):
                k = b * 3
                pool.wait_ge(stats_done, b + 1)
                pool.sem_inc(pool_past, 1)
                pool.tensor_scalar(veps[:], mv[:, :, 1], EPS, None, ALU.add).then_inc(ln_step, 1)
                pool.tensor_scalar(nmean[:], mv[:, :, 0], -1.0, None, ALU.mult).then_inc(ln_step, 1)
                pool.wait_ge(ln_step, k + 2)
                pool.sem_inc(pool_past, 1)
                pool.tensor_tensor(rstd[:], veps[:], nhalf[:], ALU.pow).then_inc(ln_step, 1)
                pool.wait_ge(ln_step, k + 3)
                pool.sem_inc(pool_past, 1)
                for qt in range(QT):
                    last = pool.tensor_scalar(xt[:, qt, :], xt[:, qt, :], nmean[:, qt:qt + 1], rstd[:, qt:qt + 1],
                                              ALU.add, ALU.mult)
                last.then_inc(xhat_ready, 1)

            def split_parts(b, c, number):
                src, made = (qf[:], ("Q", 1)) if c < 0 else (kf[c % 2][:, :, 0:CW[c]], LAST_K[c])
                buffer, here, per_batch = parts_written(c)
                out = parts[buffer][:, :, :, 0:src.shape[2]]
                n = b * st.splits + 4 * (c + 1)
                if c >= 1 or not (isinstance(b, int) and b == 0):
                    pool.wait_ge(parts_out[buffer], b * per_batch + here - len(TERMS) * 16)
                    pool.sem_inc(pool_past, 1)
                pool.wait_ge(tile_done, number(made) + 1)
                pool.sem_inc(pool_past, 1)
                r = rest[:, :, 0:src.shape[2]]
                pool.tensor_copy(out[:, 0], src).then_inc(split, 1)
                pool.wait_ge(split, n + 1)
                pool.sem_inc(pool_past, 1)
                pool.tensor_tensor(r, src, out[:, 0], ALU.subtract).then_inc(split, 1)
                pool.wait_ge(split, n + 2)
                pool.sem_inc(pool_past, 1)
                pool.tensor_copy(out[:, 1], r).then_inc(split, 1)
                pool.wait_ge(split, n + 3)
                pool.sem_inc(pool_past, 1)
                pool.tensor_tensor(out[:, 2], r, out[:, 1], ALU.subtract).then_inc(split, 1)
                pool.wait_ge(split, n + 4)
                pool.sem_inc(pool_past, 1)

            def pack_v(b, g, number):
                if number is not None:
                    pool.wait_ge(ring_free, number(LAST_V) + 1)
                    pool.sem_inc(pool_past, 1)
                if not (isinstance(b, int) and b == 0 and g < 2):
                    pool.wait_ge(pv_done, b * STEPS + (g - 1) * NK)
                    pool.sem_inc(pool_past, 1)
                for j in range(J):
                    last = pool.tensor_copy(vp[g % 2][:, :, VW * j:VW * j + D],
                                            vs[:, :, D * (J * g + j):D * (J * g + j + 1)])
                last.then_inc(v_packed, 1)

            def residual(b):
                pool.wait_ge(xres_loaded, b * 16 + 16)
                pool.sem_inc(pool_past, 1)
                for qt in range(QT):
                    last = pool.tensor_tensor(xres[:, qt, :], xres[:, qt, :], bo[:], ALU.add)
                last.then_inc(xb_ready, 1)

            def gate_exponential(b):
                pool.wait_ge(gate_step, b * GATE_STEPS + 10)
                pool.sem_inc(pool_past, 1)
                pool.tensor_tensor(top[:, 5:6], euler[:], top[:, 4:5], ALU.pow).then_inc(gate_exp, 1)

            def scale_u(b):
                pool.wait_ge(gate_step, b * GATE_STEPS + 18)
                pool.sem_inc(pool_past, 1)
                for i in range(4):
                    last = pool.tensor_scalar(uc[:, i, :], uT[:, i, :], coef[:, i:i + 1], None, ALU.mult)
                last.then_inc(uc_ready, 1)

            def keep_wo(b, number):
                pool.wait_ge(ring_free, number + 1)
                pool.sem_inc(pool_past, 1)
                pool.tensor_copy(wT["o"][:], wall[:, 3]).then_inc(wo_kept, 1)

            tile_pro = lambda op: tiles.at("prologue", op)
            job_pro = lambda op: jobs.at("prologue", op)
            layernorm(0)
            layernorm(1)
            if not cross:
                gate_exponential(0)
                scale_u(0)
            for c in range(-1, NC):
                split_parts(0, c, tile_pro)
            pack_v(0, 0, job_pro)

            def body(b):
                post, prep, ahead = flags(b)
                tile_here = lambda op: tiles.at(b, op)
                job_here = lambda op: jobs.at(b, op)
                if post:
                    residual(b - 1)
                pack_v(b, 1, None)
                if cross:
                    if prep:
                        split_parts(b + 1, -1, tile_here)
                    pack_v(b, 2, None)
                    if prep:
                        split_parts(b + 1, 0, tile_here)
                        split_parts(b + 1, 1, tile_here)
                    pack_v(b, 3, None)
                    if prep:
                        split_parts(b + 1, 2, tile_here)
                        split_parts(b + 1, 3, tile_here)
                else:
                    if prep:
                        gate_exponential(b + 1)
                    keep_wo(b, jobs.at(b, ("O", 1)) if post else job_pro(("W", 3)))
                    if prep:
                        scale_u(b + 1)
                    pack_v(b, 2, None)
                    if prep:
                        split_parts(b + 1, -1, tile_here)
                        split_parts(b + 1, 0, tile_here)
                    pack_v(b, 3, None)
                if ahead:
                    layernorm(b + 2)
                if prep:
                    pack_v(b + 1, 0, job_here)

            over_batches(pool, body)
            residual(B - 1)


def flamingo_layer(nc, x, ctxT, wx, we, y, out):
    def parts(name, n):
        return nc.dram_tensor(name, (2 * G, len(TERMS), D, 2, n), BF16, kind="Internal").ap()

    with ExitStack() as sems:
        run_stage(nc, Stage(True), sems, x, y, ctxT, wx, (parts("cross_q", T), parts("cross_k", KEYS)), "cross")
        run_stage(nc, Stage(False), sems, y, out, None, we, (parts("expert_q", T), parts("expert_k", T)), "expert")


def kernel(**inputs):
    import numpy as np
    import concourse.bacc as bacc
    from concourse.bass_utils import run_bass_kernel_spmd

    a = {n: np.asarray(v) for n, v in inputs.items()}

    def rows(v, n=128):
        return np.broadcast_to(v.reshape(1, -1), (n, v.size))

    def column(v):
        return v.reshape(-1, 128).T

    def paired(v):
        shape = v.shape[:-1]
        v = v.reshape(*shape, 2 * G, 2, D)
        return np.moveaxis(v, -2, -3).reshape(*shape, C)

    f, c = "L0_ffn_", "L0_xattn_"
    names = ("q", "k", "v", "o")
    data = {"x": a["x"], "ctxT": a["ctx_1024"].transpose(0, 2, 1)}
    wx = {"w" + n: a[c + "W" + n].T for n in names}
    wx |= {"bv": rows(a[c + "bv"]), "bo": rows(a[c + "bo"]),
           "gate": rows(a["g_xattn"])}
    we = {"w" + n: a[f + n + "Wm"].T for n in names}
    for d, bq, bk in ((wx, a[c + "bq"], a[c + "bk"]), (we, a[f + "qb"], a[f + "kb"])):
        d |= {"wq": paired(d["wq"]), "wk": paired(d["wk"]), "bq": column(paired(bq)), "bk": column(paired(bk))}
    we |= {"u": np.stack([(paired if n in "qk" else np.asarray)(a[f + n + "U"].transpose(0, 2, 1).reshape(EX * RANK, C))
                          for n in names]),
           "v": np.stack([a[f + n + "V"].reshape(EX * RANK, C) for n in names]),
           "s": np.stack([a[f + n + "S"].reshape(EX * RANK) for n in names], 1),
           "bv": rows(a[f + "vb"]), "bo": rows(a[f + "ob"]),
           "gate": rows(a["g_ffn"]), "gw1": a[f + "gw1"].T, "gw2": a[f + "gw2"].T,
           "gb1": a[f + "gb1"].reshape(-1, 1), "gb2": a[f + "gb2"].reshape(1, -1)}
    data |= {"x_" + n: v for n, v in wx.items()} | {"e_" + n: v for n, v in we.items()}

    nc = bacc.Bacc("TRN2", target_bir_lowering=False, num_devices=1)
    arrays, aps = {}, {}
    for name, v in data.items():
        arrays[f"in_{name}"] = np.ascontiguousarray(v)
        aps[name] = nc.dram_tensor(f"in_{name}", v.shape, mybir.dt.from_np(v.dtype), kind="ExternalInput").ap()
    y = nc.dram_tensor("after_cross", (B, T, C), F32, kind="Internal").ap()
    out = nc.dram_tensor("out", (B, T, C), F32, kind="ExternalOutput").ap()
    flamingo_layer(nc, aps["x"], aps["ctxT"], {n: aps["x_" + n] for n in wx}, {n: aps["e_" + n] for n in we}, y, out)
    r = run_bass_kernel_spmd(nc, [arrays], core_ids=[0])
    return r.results[0]["out"]
```

```python
from contextlib import ExitStack

import concourse.bass as bass
from concourse import mybir

F32 = mybir.dt.float32
BF16 = mybir.dt.bfloat16
ALU = mybir.AluOpType
ACT = mybir.ActivationFunctionType
AX = mybir.AxisListType

B, T, C = 16, 512, 256
KEYS = 1601
H, D = 16, 16
G, J = 4, 4
QT = T // 128
CC = C // 128
EX, RANK, GH = 8, 16, 64
VW = D + 1
VPAD = J * VW + 32 - VW
EPS = 1e-5
QSCALE = float(D) ** -0.5
TERMS = [(0, 0), (0, 1), (1, 0), (1, 1), (0, 2), (2, 0)]
KROWS = [99, 128]
FILL_DMAS = 6
NPROB = 4


class Ring:

    def __init__(self, depth, plans, members):
        pick = lambda ops: {op: n for n, op in enumerate(op for op in ops if op[0] in members)}
        self.depth = depth
        self.loc = {kind: pick(ops) for kind, ops in plans.items()}
        self.per_iter = len(self.loc["mid"])
        assert self.per_iter % depth == 0

    def base(self, b):
        size = {kind: len(uses) for kind, uses in self.loc.items()}
        start = size["opening"] + size["prologue"]
        if isinstance(b, str):
            return {"opening": 0, "prologue": size["opening"]}[b] if b != "tail" else self.base(B - 1) + size["last"]
        if isinstance(b, int) and b == 0:
            return start
        if isinstance(b, int) and b == B - 1:
            return self.base(B - 2) + size["nearly"]
        return b * self.per_iter + (start + size["first"] - self.per_iter)

    def uses(self, b):
        return self.loc[kind_of(b)]

    def at(self, b, op):
        return self.base(b) + self.uses(b)[op]

    def slot(self, b, op):
        return self.at(b if isinstance(b, (int, str)) else 1, op) % self.depth

    def before(self, b, op):
        if isinstance(b, int):
            return self.at(b - 1 if b else "prologue", op)
        return self.base(b) + (self.loc["mid"][op] - self.per_iter)


def kind_of(b):
    if isinstance(b, str):
        return b
    if isinstance(b, int):
        return {0: "first", B - 2: "nearly", B - 1: "last"}.get(b, "mid")
    return "mid"


class Stage:

    def __init__(self, cross):
        self.cross = cross
        self.keys = KEYS if cross else T
        self.nk = -(-self.keys // 128)
        self.kr = [min(128, self.keys - 128 * k) for k in range(self.nk)]
        self.nc = -(-self.keys // 512)
        self.cw = [min(512, self.keys - 512 * c) for c in range(self.nc)]
        self.k_tiles = [("K", c, m) for c in range(self.nc) for m in ((0, 1) if self.cw[c] > 256 else (2,))]
        self.v_jobs = [(0, 2), (2, 4), (4, 6), (6, 8), (8, 10), (10, 11), (11, 12), (12, 13)] if cross else [(0, 4)]
        self.splits = 4 + 4 * self.nc
        q, v = [("Q", 0), ("Q", 1)], [("V", i) for i in range(len(self.v_jobs))]
        gates = [] if cross else [("h",), ("lg",), ("gb",), ("coef",)]
        w = [] if cross else [("W", i) for i in range(4)]
        opening = [("xT", 0), ("xT", 1)] + gates
        here = self.place()
        self.plans = {
            "opening": opening,
            "prologue": w + q + self.k_tiles + v + [("stats",)] + opening + self.maxima(0)
                        + [("MS", 0), ("M", 0)] + self.early,
            "first": self.iteration(here, False, True, True),
            "mid": self.iteration(here, True, True, True),
            "nearly": self.iteration(here, True, True, False),
            "last": self.iteration(here, True, False, False),
            "tail": [("OT", G - 1), ("aT", 0), ("aT", 1), ("O", 0), ("O", 1)],
        }
        self.tiles = Ring(3, self.plans, ("S", "M", "xT", "aT", "Q", "K", "h", "gb"))
        self.jobs = Ring(2, self.plans, ("max", "OT", "O", "V", "lg", "W"))

    def maxima(self, g):
        whole = [c for c in range(self.nc) if self.cw[c] == 512]
        rest = [c for c in range(self.nc) if self.cw[c] < 512]
        return [op for hp in range(2) for op in [("max", g, hp, qt, c) for qt in range(QT) for c in whole]
                + [("max", g, hp, None, c) for c in rest]]

    def place(self):
        k, n = self.k_tiles, self.nk * J
        if self.cross:
            at = [
                [(2, ("Q", 0)), (6, ("Q", 1)), (9, ("OT", 3)), (13, ("aT", 0)), (14, ("aT", 1)),
                 (18, ("O", 0)), (24, k[0]), (30, k[1]), (36, ("O", 1)), (43, k[2])],
                [(0, k[3]), (9, ("OT", 0)), (14, k[4]), (24, k[5]), (34, k[6]), (46, ("stats",))],
                [(8, ("V", 0)), (9, ("OT", 1)), (18, ("V", 1)), (27, ("V", 2)), (36, ("V", 3)), (46, ("V", 4))],
                [(4, ("V", 5)), (9, ("OT", 2)), (15, ("V", 6)), (25, ("V", 7)), (30, ("xT", 0)), (31, ("xT", 1))],
            ]
            final, m_at = 38, 46
        else:
            at = [
                [(1, ("W", 0)), (2, ("W", 1)), (3, ("Q", 0)), (5, ("OT", 3)), (6, ("Q", 1)), (7, ("aT", 0)), (8, ("aT", 1)),
                 (10, k[0]), (15, k[1])],
                [(2, ("W", 2)), (5, ("OT", 0)), (9, ("O", 0)), (12, ("stats",))],
                [(1, ("O", 1)), (5, ("OT", 1)), (7, ("W", 3)), (8, ("V", 0)), (11, ("xT", 0)), (12, ("xT", 1)), (14, ("h",)),
                 (15, ("lg",))],
                [(5, ("OT", 2)), (7, ("gb",)), (9, ("coef",))],
            ]
            final, m_at = 8, 14
        here = [[] for _ in range(G * n)]
        for g in range(G):
            for i, op in at[g]:
                here[g * n + i].append(op)
            here[g * n + final].append(("MS", (g + 1) % G))
            here[g * n + m_at].append(("M", (g + 1) % G))
        self.early = []
        for g in range(G):
            window = [i % (G * n) for i in range(g * n + final, (g + 1) * n + final)]
            mx = self.maxima((g + 2) % G)
            ops = [op for i in window for op in here[i]] + mx
            until = n * 2 * T + sum(self.tensor_cost(op) for op in ops)
            work = sum(self.vector_cost(op) for op in ops)
            tensor = vector = 0
            for i in window:
                for op in here[i]:
                    tensor += self.tensor_cost(op)
                    vector += self.vector_cost(op)
                while mx and vector * until <= work * tensor:
                    here[i].append(mx.pop(0))
                    tensor += self.tensor_cost(here[i][-1])
                    vector += self.vector_cost(here[i][-1])
                    if g == G - 1 and i >= G * n - (n - final):
                        self.early.append(here[i][-1])
                tensor += 2 * T
            before = here[(window[-1] + 1) % (G * n)]
            before[0:0] = mx
        return here

    def iteration(self, here, post, prep, ahead):
        there = {-1: post, 0: True, 1: prep, 2: ahead}
        out = []
        for i, ops in enumerate(here):
            s, j = divmod(i, J)
            out += [op for op in ops if there[self.batch_of(0, op)]]
            out.append(("S", s // self.nk, s % self.nk, j))
            if j == J - 1:
                if s or post:
                    out.append(("PV", (s - 1) % (G * self.nk)))
                if s % self.nk == 0 and (s or post):
                    out.append(("HC", (s // self.nk - 1) % G))
        return out

    def batch_of(self, b, op):
        if op[0] in ("aT", "O") or op == ("OT", G - 1):
            return b - 1
        if op[0] in ("OT", "S") or (op[0] in ("max", "M", "MS") and op[1] > 0 and op not in self.early):
            return b
        if op[0] in ("xT", "h", "lg", "gb", "coef", "stats"):
            return b + 2
        return b + 1

    def tensor_cost(self, op):
        if op[0] == "max":
            return 2 * self.cw[op[4]] * (1 if op[3] is not None else QT)
        if op[0] == "K":
            return 2 * 4 * self.cw[op[1]] * (2 if op[2] == 2 else 1)
        return {"V": 4096, "Q": 4096, "O": 4096, "W": 2048}.get(op[0], 512)

    def vector_cost(self, op):
        if op[0] == "max":
            return self.tensor_cost(op) + 220
        return {"V": 730, "OT": 1000, "O": 730, "W": 730, "lg": 3000}.get(op[0], 0)


def run_stage(nc, st, sems, x_in, x_out, ctxT, w, stacks, tag):
    cross, NK, NC, KR, CW = st.cross, st.nk, st.nc, st.kr, st.cw
    tiles, jobs = st.tiles, st.jobs
    NT = J * NK
    STEPS = G * NK
    LAST_V = ("V", len(st.v_jobs) - 1)
    LAST_K = {c: [k for k in st.k_tiles if k[1] == c][-1] for c in range(NC)}
    ctx = ExitStack()
    with ctx:
        def sb(name, shape, dt=F32):
            return ctx.enter_context(nc.sbuf_tensor(f"{tag}_{name}", shape, dt))

        def sem(name):
            return sems.enter_context(nc.semaphore(f"{tag}_{name}"))

        ring = [ctx.enter_context(nc.psum_tensor(f"{tag}_ring{i}", [128, 2, 512], F32)) for i in range(2)]
        tile = [ctx.enter_context(nc.psum_tensor(f"{tag}_tile{i}", [128, 512], F32)) for i in range(3)]
        heads = ctx.enter_context(nc.psum_tensor(f"{tag}_heads", [128, 512], F32))

        xt = sb("xt", [128, QT, C])
        xT = sb("xT", [128, CC, T])
        xres = sb("xres", [128, QT, C])
        xo = sb("xo", [128, QT, C])
        qf = sb("qf", [128, CC, T])
        kf = [sb(f"kf{i}", [128, CC, 512]) for i in range(2)]
        rest = sb("rest", [128, CC, 512])
        parts = [sb(f"parts{i}", [128, 3, CC, 512], BF16) for i in range(2)]
        kst = sb("kst", [128, G, J, st.keys], BF16)
        qst = sb("qst", [128, G, J, T], BF16)
        vs = sb("vs", [128, NK, C])
        vp = [sb(f"vp{i}", [128, NK, VPAD]) for i in range(2)]
        prob = [sb(f"prob{i}", [128, J, T]) for i in range(NPROB)]
        hsb = sb("hsb", [128, T])
        attn = sb("attn", [128, QT, C])
        attnT = sb("attnT", [128, CC, T])
        rden = sb("rden", [128, QT, J])
        stats = sb("stats", [128, QT, 6])
        mv = sb("mv", [128, QT, 2])
        veps = sb("veps", [128, QT])
        nmean = sb("nmean", [128, QT])
        rstd = sb("rstd", [128, QT])
        nhalf = sb("nhalf", [128, QT])
        mxp = sb("mxp", [128, 2 * QT, 2, NC])
        negm = sb("negm", [128, 2 * QT, 2])
        mrest = sb("mrest", [128, 2 * QT, 2])
        mparts = sb("mparts", [128, 2 * QT, 128], BF16)
        ident = sb("ident", [128, 128])
        identb = sb("identb", [128, 128], BF16)
        bq = sb("bq", [128, CC])
        bk = sb("bk", [128, CC])
        bv = sb("bv", [128, C])
        bo = sb("bo", [128, C])
        gate = sb("gate", [128, 1])
        weights = ["q", "k", "v", "o"]
        if cross:
            cT = sb("cT", [128, CC, KEYS])
            wT = {n: sb(f"w{n}", [128, CC, C]) for n in weights}
        else:
            cT = xT
            wall = sb("wall", [128, 4, CC, C])
            wT = {n: wall[:, i] for i, n in enumerate(weights)}
            wT["o"] = sb("wo_now", [128, CC, C])
            wm = sb("wm", [128, 4, CC, C])
            uT = sb("uT", [128, 4, C])
            vw = sb("vw", [128, 4, C])
            uc = sb("uc", [128, 4, C])
            sv = sb("sv", [128, 4])
            coef = sb("coef", [128, 4])
            gw1 = sb("gw1", [128, CC, GH])
            gw2 = sb("gw2", [GH, EX])
            gb1 = sb("gb1", [GH, 1])
            gb2 = sb("gb2", [1, EX])
            prio = sb("prio", [1, EX])
            onehot = sb("onehot", [128, EX])
            ones = sb("ones", [1, 128])
            euler = sb("euler", [1, 1])
            pooled = sb("pooled", [128, CC])
            hid = sb("hid", [GH, 1])
            lg = sb("lg", [1, EX])
            lg2 = sb("lg2", [1, EX])
            top = sb("top", [1, 8])
            cand = sb("cand", [1, 2, EX])
            pick = sb("pick", [1, 2, EX])
            gates = sb("gates", [1, 2, EX])
            gsel = sb("gsel", [128, EX])
            gsb = sb("gsb", [128, EX])
            csum = sb("csum", [128, 1])

        pool_past, sp_past, dve_past, pe_past = (sem(f"{e}_past") for e in ("pool", "sp", "dve", "pe"))
        w_loaded = sem("w_loaded")
        const_dve = sem("const_dve")
        const_pool = sem("const_pool")
        rows_set = sem("rows_set")
        gate_tanh = sem("gate_tanh")
        x_loaded = sem("x_loaded")
        ctx_loaded = sem("ctx_loaded")
        xres_loaded = sem("xres_loaded")
        fill_done = [sem(f"fill_done{g}") for g in range(G)]
        parts_out = [sem(f"parts_out{i}") for i in range(2)]
        stored = sem("stored")
        ring_full = sem("ring_full")
        ring_free = sem("ring_free")
        tile_full = sem("tile_full")
        tile_done = sem("tile_done")
        pv_done = sem("pv_done")
        heads_copied = sem("heads_copied")
        stats_done = sem("stats_done")
        stats_step = sem("stats_step")
        ln_step = sem("ln_step")
        xhat_ready = sem("xhat_ready")
        xb_ready = sem("xb_ready")
        split = sem("split")
        v_packed = sem("v_packed")
        m_step = sem("m_step")
        den_ready = sem("den_ready")
        if not cross:
            gate_step = sem("gate_step")
            gate_exp = sem("gate_exp")
            uc_ready = sem("uc_ready")
            wo_kept = sem("wo_kept")
        GATE_STEPS = 18
        CONST_DVE, CONST_POOL = (8, 3) if cross else (9, 8 + EX)
        block = ctx.enter_context(nc.Block())

        x_rows = x_in.rearrange("b (p t) c -> b p t c", t=QT)
        out_rows = x_out.rearrange("b (p t) c -> b p t c", t=QT)
        n_weights = 9 if cross else 16

        def over_batches(engine, body):
            body(0)
            with engine.Fori(1, B - 2) as b:
                body(b)
            body(B - 2)
            body(B - 1)

        def flags(b):
            known = isinstance(b, int)
            return not (known and b == 0), not (known and b == B - 1), not (known and b >= B - 2)

        def parts_written(c):
            buffer = (c + 1) % 2
            here = len([x for x in range(-1, c + 1) if (x + 1) % 2 == buffer])
            per_batch = len([x for x in range(-1, NC) if (x + 1) % 2 == buffer])
            return buffer, here * len(TERMS) * 16, per_batch * len(TERMS) * 16

        def split_parts(eng, past, b, c, number):
            src, made = (qf[:], ("Q", 1)) if c < 0 else (kf[c % 2][:, :, 0:CW[c]], LAST_K[c])
            buffer, here, per_batch = parts_written(c)
            out = parts[buffer][:, :, :, 0:src.shape[2]]
            n = b * st.splits + 4 * (c + 1)
            if c >= 1 or not (isinstance(b, int) and b == 0):
                eng.wait_ge(parts_out[buffer], b * per_batch + here - len(TERMS) * 16)
                eng.sem_inc(past, 1)
            eng.wait_ge(tile_done, number(made) + 1)
            eng.sem_inc(past, 1)
            r = rest[:, :, 0:src.shape[2]]
            eng.tensor_copy(out[:, 0], src).then_inc(split, 1)
            eng.wait_ge(split, n + 1)
            eng.sem_inc(past, 1)
            eng.tensor_tensor(r, src, out[:, 0], ALU.subtract).then_inc(split, 1)
            eng.wait_ge(split, n + 2)
            eng.sem_inc(past, 1)
            eng.tensor_copy(out[:, 1], r).then_inc(split, 1)
            eng.wait_ge(split, n + 3)
            eng.sem_inc(past, 1)
            eng.tensor_tensor(out[:, 2], r, out[:, 1], ALU.subtract).then_inc(split, 1)
            eng.wait_ge(split, n + 4)
            eng.sem_inc(past, 1)

        @block.sync
        def _(sp):
            loads = []
            if cross:
                loads += [(wT[n][:], w["w" + n].rearrange("(c p) o -> p c o", p=128)) for n in weights]
                loads += [(bo[:], w["bo"]), (bv[:], w["bv"]), (bq[:], w["bq"]), (bk[:], w["bk"]), (gate[:], w["gate"])]
            else:
                loads += [(wm[:, i], w["w" + n].rearrange("(c p) o -> p c o", p=128)) for i, n in enumerate(weights)]
                loads += [(uT[:], w["u"].rearrange("n p o -> p n o")), (vw[:], w["v"].rearrange("n p o -> p n o")),
                          (sv[:], w["s"]), (bo[:], w["bo"]), (bv[:], w["bv"]), (bq[:], w["bq"]), (bk[:], w["bk"]),
                          (gate[:], w["gate"]), (gw1[:], w["gw1"].rearrange("(c p) o -> p c o", p=128)),
                          (gw2[:], w["gw2"]), (gb1[:], w["gb1"]), (gb2[:], w["gb2"])]
            assert len(loads) == n_weights
            sp.dma_start(xt[:], x_rows[0]).then_inc(x_loaded, 16)
            for dst, src in loads:
                sp.dma_start(dst, src).then_inc(w_loaded, 16)
            if cross:
                sp.dma_start(cT[:], ctxT[0].rearrange("(c p) k -> p c k", p=128)).then_inc(ctx_loaded, 16)

            qd, kd = stacks

            def write_parts(b, c):
                buffer = (c + 1) % 2
                width = T if c < 0 else CW[c]
                cols = slice(0, T) if c < 0 else slice(512 * c, 512 * c + CW[c])
                which = 0 if c < 0 else 1
                dst = qd if c < 0 else kd
                for part, step in ((0, 1), (1, 3), (2, 4)):
                    sp.wait_ge(split, b * st.splits + 4 * (c + 1) + step)
                    sp.sem_inc(sp_past, 1)
                    for s, term in enumerate(TERMS):
                        if term[which] == part:
                            sp.dma_start(dst[:, s, :, :, cols], parts[buffer][:, part, :, 0:width])\
                                .then_inc(parts_out[buffer], 16)

            def parts_in_dram(b):
                for c in (NC - 2, NC - 1):
                    buffer, here, per_batch = parts_written(c)
                    sp.wait_ge(parts_out[buffer], b * per_batch + here)
                    sp.sem_inc(sp_past, 1)

            def stacks_read(b):
                for g in range(G):
                    sp.wait_ge(fill_done[g], b * (FILL_DMAS * 16))
                    sp.sem_inc(sp_past, 1)

            def fill(b, g):
                if not (isinstance(b, int) and b == 0):
                    sp.wait_ge(tile_full, last_score(b, g) + 1)
                for stack, src in ((qst, qd), (kst, kd)):
                    sp.dma_start(stack[0:96, g, 0:2, :], src[2 * g].rearrange("s d h n -> (s d) h n"))\
                        .then_inc(fill_done[g], 16)
                    sp.dma_start(stack[64:128, g, 2:4, :], src[2 * g + 1, 0:4].rearrange("s d h n -> (s d) h n"))\
                        .then_inc(fill_done[g], 16)
                    sp.dma_start(stack[0:32, g, 2:4, :], src[2 * g + 1, 4:6].rearrange("s d h n -> (s d) h n"))\
                        .then_inc(fill_done[g], 16)

            def last_score(b, g):
                if isinstance(b, int):
                    return tiles.at(b - 1, ("S", g, NK - 1, J - 1))
                return tiles.base(b) + (tiles.loc["mid"][("S", g, NK - 1, J - 1)] - tiles.per_iter)

            sp.wait_ge(tile_done, tiles.at("opening", ("xT", 1)) + 1)
            sp.dma_start(xt[:], x_rows[1]).then_inc(x_loaded, 16)
            for c in range(-1, NC):
                write_parts(0, c)
            parts_in_dram(0)
            for g in range(3):
                sp.wait_ge(rows_set, 4 * (g + 1))
                fill(0, g)
            sp.wait_ge(rows_set, 4 * G)

            def body(b):
                post, prep, ahead = flags(b)
                if ahead:
                    sp.wait_ge(tile_done, tiles.before(b, ("xT", 1)) + 1)
                    sp.sem_inc(sp_past, 1)
                    sp.dma_start(xt[:], x_rows[b + 2]).then_inc(x_loaded, 16)
                if post:
                    if not isinstance(b, int) or b > 1:
                        sp.wait_ge(ring_free, jobs.before(b, ("O", 1)) + 1)
                        sp.sem_inc(sp_past, 1)
                    sp.dma_start(xres[:], x_rows[b - 1]).then_inc(xres_loaded, 16)
                if prep and cross:
                    sp.wait_ge(ring_free, jobs.before(b, LAST_V) + 1)
                    sp.sem_inc(sp_past, 1)
                    sp.dma_start(cT[:], ctxT[b + 1].rearrange("(c p) k -> p c k", p=128)).then_inc(ctx_loaded, 16)
                fill(b, 3)
                if prep:
                    stacks_read(b + 1)
                    for c in range(-1, NC):
                        write_parts(b + 1, c)
                    parts_in_dram(b + 1)
                    for g in range(2):
                        fill(b + 1, g)
                if post:
                    sp.wait_ge(ring_free, jobs.at(b, ("O", 1)) + 1)
                    sp.sem_inc(sp_past, 1)
                    sp.dma_start(out_rows[b - 1], xo[:]).then_inc(stored, 16)
                if prep:
                    fill(b + 1, 2)

            over_batches(sp, body)
            sp.wait_ge(ring_free, jobs.at(B - 1, ("O", 1)) + 1)
            sp.dma_start(xres[:], x_rows[B - 1]).then_inc(xres_loaded, 16)
            sp.wait_ge(ring_free, jobs.at("tail", ("O", 1)) + 1)
            sp.dma_start(out_rows[B - 1], xo[:]).then_inc(stored, 16)
            sp.wait_ge(stored, 16 * B)

        @block.tensor
        def _(pe):
            def slot_free(where, ring, op, done, after=None):
                base, loc = ring.base(where), ring.uses(where)
                least = max(loc[op] - ring.depth + 1, loc[after] + 1 if after else -10 ** 9)
                if not isinstance(base, int) or base + least > 0:
                    pe.wait_ge(done, base + least)

            def job(where, b, op):
                slot, kind = ring[jobs.slot(where, op)], op[0]
                slot_free(where, jobs, op, ring_free, ("W", 2) if kind == "V" and not cross else None)
                if kind == "max":
                    _, g, hp, qt, c = op
                    pe.wait_ge(fill_done[g], b * (FILL_DMAS * 16) + FILL_DMAS * 16)
                    for i, qt in enumerate([qt] if qt is not None else range(QT)):
                        for e in range(2):
                            j, r = 2 * e + hp, 64 * e
                            mm = pe.matmul(slot[:, 1 - e, i * CW[c]:(i + 1) * CW[c]],
                                           qst[r:r + 64, g, j, 128 * qt:128 * qt + 128],
                                           kst[r:r + 64, g, j, 512 * c:512 * c + CW[c]], start=True, stop=True)
                elif kind == "OT":
                    pe.wait_ge(heads_copied, b * G + op[1] + 1)
                    for qt in range(QT):
                        mm = pe.transpose(slot[:, 0, 128 * qt:128 * qt + 128], hsb[:, 128 * qt:128 * qt + 128], ident[:])
                elif kind == "O":
                    pe.wait_ge(tile_done, tiles.at(where, ("aT", 1)) + 1)
                    if not cross:
                        pe.wait_ge(wo_kept, b + 1)
                    for i in range(2):
                        qt = 2 * op[1] + i
                        for c in range(CC):
                            mm = pe.matmul(slot[:, 0, 256 * i:256 * i + 256], attnT[:, c, 128 * qt:128 * qt + 128],
                                           wT["o"][:, c, :], start=(c == 0), stop=(c == CC - 1))
                elif kind == "V":
                    k0, k1 = st.v_jobs[op[1]]
                    if cross:
                        pe.wait_ge(ctx_loaded, b * 16 + 16)
                    for i, kt in enumerate(range(k0, k1)):
                        for c in range(CC):
                            mm = pe.matmul(slot[0:KR[kt], i // 2, 256 * (i % 2):256 * (i % 2) + 256],
                                           cT[:, c, 128 * kt:128 * kt + KR[kt]], wT["v"][:, c, :],
                                           start=(c == 0), stop=(c == CC - 1))
                elif kind == "lg":
                    pe.wait_ge(tile_done, tiles.at(where, ("h",)) + 1)
                    pe.sem_inc(pe_past, 1)
                    mm = pe.matmul(slot[0:1, 0, 0:EX], hid[:], gw2[:], start=True, stop=True)
                elif kind == "W":
                    pe.wait_ge(uc_ready, b + 1)
                    for c in range(CC):
                        mm = pe.matmul(slot[:, 0, 256 * c:256 * c + 256], vw[:, op[1], 128 * c:128 * c + 128],
                                       uc[:, op[1], :], start=True, stop=True)
                mm.then_inc(ring_full, 1)

            def tile_use(where, b, op):
                n, kind = tiles.slot(where, op), op[0]
                bank = tile[n]
                slot_free(where, tiles, op, tile_done, {"h": ("xT", 1)}.get(kind))
                if kind == "S":
                    _, g, kt, j = op
                    if isinstance(b, int) and (b, g, kt) == (0, 0, 0):
                        pe.wait_ge(tile_done, tiles.at("prologue", ("M", 0)) + 1)
                    rows = KROWS[j // 2]
                    mm = pe.matmul(bank[0:KR[kt], :], kst[0:rows, g, j, 128 * kt:128 * kt + KR[kt]],
                                   qst[0:rows, g, j, :], start=True, stop=True)
                elif kind == "M":
                    pe.wait_ge(m_step, b * (5 * G) + 5 * (op[1] + 1))
                    for i in range(2 * QT):
                        mm = pe.transpose(bank[:, 64 * i:64 * i + 64].bitcast(BF16), mparts[:, i, :], identb[:])
                elif kind in ("xT", "aT"):
                    if kind == "xT":
                        pe.wait_ge(xhat_ready, b + 1)
                    else:
                        pe.wait_ge(ring_free, jobs.at(where, ("OT", G - 1)) + 1)
                    src, c = (xt if kind == "xT" else attn), op[1]
                    for qt in range(QT):
                        mm = pe.transpose(bank[:, 128 * qt:128 * qt + 128], src[:, qt, 128 * c:128 * c + 128], ident[:])
                elif kind == "Q":
                    if cross and kind_of(where) == "prologue":
                        pe.wait_ge(tile_done, tiles.at("opening", ("xT", 1)) + 1)
                    if not cross:
                        pe.wait_ge(ring_free, jobs.at(where, ("W", 0)) + 1)
                    m = op[1]
                    for c in range(CC):
                        mm = pe.matmul(bank[:, :], wT["q"][:, c, 128 * m:128 * m + 128], xT[:, c, :],
                                       start=(c == 0), stop=(c == CC - 1))
                elif kind == "K":
                    _, k, which = op
                    if cross:
                        pe.wait_ge(ctx_loaded, b * 16 + 16)
                    else:
                        pe.wait_ge(ring_free, jobs.at(where, ("W", 1)) + 1)
                    for m in ((0, 1) if which == 2 else (which,)):
                        out = bank[:, CW[k] * m:CW[k] * (m + 1)] if which == 2 else bank[:, 0:CW[k]]
                        for c in range(CC):
                            mm = pe.matmul(out, wT["k"][:, c, 128 * m:128 * m + 128],
                                           cT[:, c, 512 * k:512 * k + CW[k]], start=(c == 0), stop=(c == CC - 1))
                elif kind == "h":
                    for c in range(CC):
                        mm = pe.matmul(bank[0:GH, 0:1], gw1[:, c, :], pooled[:, c:c + 1],
                                       start=(c == 0), stop=(c == CC - 1))
                elif kind == "gb":
                    pe.wait_ge(gate_step, b * GATE_STEPS + 15)
                    mm = pe.matmul(bank[:, 0:EX], ones[:], gates[:, 1, :], start=True, stop=True)
                mm.then_inc(tile_full, 1)

            def pv_step(b, s, exps):
                g, kt = divmod(s, NK)
                pe.wait_ge(tile_done, exps + 1)
                if kt == 0:
                    pe.wait_ge(v_packed, b * G + g + 1)
                    if not (isinstance(b, int) and b == 0 and g == 0):
                        pe.wait_ge(heads_copied, b * G + g)
                for j in range(J):
                    mm = pe.matmul(heads[32 * j:32 * j + 32, :], vp[g % 2][0:KR[kt], kt, VW * j:VW * j + 32],
                                   prob[s % NPROB][0:KR[kt], j, :], start=(kt == 0), stop=(kt == NK - 1))
                mm.then_inc(pv_done, 1)

            pe.wait_ge(w_loaded, 16 * n_weights)
            pe.wait_ge(const_dve, CONST_DVE)
            pe.wait_ge(const_pool, CONST_POOL)

            def one(where, b, op):
                if op in jobs.uses(where):
                    job(where, b, op)
                elif op in tiles.uses(where):
                    tile_use(where, b, op)

            for b, where in ((-2, "opening"), (-1, "prologue")):
                for op in st.plans[where]:
                    one(where, st.batch_of(b, op), op)

            def body(b):
                for op in st.plans[kind_of(b)]:
                    if op[0] != "PV":
                        one(b, st.batch_of(b, op), op)
                    elif op[1] < STEPS - 1:
                        pv_step(b, op[1], tiles.at(b, ("S", *divmod(op[1], NK), J - 1)))
                    else:
                        pv_step(b - 1, STEPS - 1, tiles.base(b) - 1)

            over_batches(pe, body)
            pv_step(B - 1, STEPS - 1, tiles.base("tail") - 1)
            for op in st.plans["tail"]:
                one("tail", B - 1, op)

        @block.scalar
        def _(act):
            act.wait_ge(w_loaded, 16 * n_weights)
            act.activation(gate[:], gate[:], ACT.Tanh).then_inc(gate_tanh, 1)
            act.wait_ge(const_dve, CONST_DVE)
            act.wait_ge(const_pool, CONST_POOL)

            def tile_use(where, b, op):
                bank, kind = tile[tiles.slot(where, op)], op[0]
                if kind == "S":
                    _, g, kt, j = op
                    s = g * NK + kt
                    if j == 0 and not (isinstance(b, int) and b == 0 and s < NPROB):
                        act.wait_ge(pv_done, b * STEPS + s - NPROB + 1)
                    act.wait_ge(tile_full, tiles.at(where, op) + 1)
                    done = act.activation(prob[s % NPROB][0:KR[kt], j, :], bank[0:KR[kt], :], ACT.Exp)
                    done.then_inc(tile_done, 1)
                    return
                if kind == "Q" or kind == "K":
                    c = op[1]
                    if kind == "K" and c >= 2:
                        act.wait_ge(split, b * st.splits + 4 + 4 * (c - 2) + 2)
                    elif not (isinstance(b, int) and b == 0):
                        act.wait_ge(split, b * st.splits)
                act.wait_ge(tile_full, tiles.at(where, op) + 1)
                if kind == "M":
                    g = op[1]
                    seen = bank[:, :].bitcast(BF16).rearrange("p (h q) -> p h q", h=2)
                    act.activation(qst[32:64, g, 2:4, :], seen[32:64], ACT.Copy)
                    done = act.activation(qst[96:99, g, 0:2, :], seen[96:99], ACT.Copy)
                elif kind == "aT":
                    done = act.activation(attnT[:, op[1], :], bank[:, :], ACT.Copy)
                elif kind == "xT" and cross:
                    done = act.activation(xT[:, op[1], :], bank[:, :], ACT.Copy)
                elif kind == "xT":
                    done = act.activation(xT[:, op[1], :], bank[:, :], ACT.Copy, accum_out=pooled[:, op[1]:op[1] + 1])
                elif kind == "Q":
                    m = op[1]
                    done = act.activation(qf[:, m, :], bank[:, :], ACT.Identity, bias=bq[:, m:m + 1], scale=QSCALE)
                elif kind == "K":
                    _, c, which = op
                    for m in ((0, 1) if which == 2 else (which,)):
                        src = bank[:, CW[c] * m:CW[c] * (m + 1)] if which == 2 else bank[:, 0:CW[c]]
                        done = act.activation(kf[c % 2][:, m, 0:CW[c]], src, ACT.Identity, bias=bk[:, m:m + 1])
                elif kind == "h":
                    done = act.activation(hid[:], bank[0:GH, 0:1], ACT.Relu, bias=gb1[:], scale=1.0 / T)
                elif kind == "gb":
                    done = act.activation(gsb[:], bank[:, 0:EX], ACT.Copy)
                done.then_inc(tile_done, 1)

            def copy_heads(b, g, last_ot):
                act.wait_ge(pv_done, b * STEPS + (g + 1) * NK)
                if last_ot is not None:
                    act.wait_ge(ring_full, last_ot + 1)
                act.activation(hsb[:], heads[:], ACT.Copy).then_inc(heads_copied, 1)

            for b, where in ((-2, "opening"), (-1, "prologue")):
                for op in tiles.uses(where):
                    tile_use(where, st.batch_of(b, op), op)

            def body(b):
                post, _, _ = flags(b)
                for op in st.plans[kind_of(b)]:
                    if op in tiles.uses(b):
                        tile_use(b, st.batch_of(b, op), op)
                    elif op == ("HC", G - 1):
                        copy_heads(b - 1, G - 1, jobs.before(b, ("OT", G - 2)))
                    elif op[0] == "HC":
                        g = op[1]
                        copy_heads(b, g, jobs.at(b, ("OT", (g - 1) % G)) if g or post else None)

            over_batches(act, body)
            copy_heads(B - 1, G - 1, jobs.at(B - 1, ("OT", G - 2)))
            for op in tiles.uses("tail"):
                tile_use("tail", B - 1, op)

        @block.vector
        def _(dve):
            def layernorm_stats(b):
                dve.wait_ge(x_loaded, b * 16 + 16)
                if not isinstance(b, int) or b > 0:
                    dve.wait_ge(xhat_ready, b)
                for qt in range(QT):
                    last = dve.bn_stats(stats[:, qt, :], xt[:, qt, :])
                last.then_inc(stats_step, 1)
                dve.wait_ge(stats_step, b + 1)
                dve.sem_inc(dve_past, 1)
                for qt in range(QT):
                    last = dve.bn_aggr(mv[:, qt, :], stats[:, qt, :])
                last.then_inc(stats_done, 1)

            dve.memset(vs[:], 0.0).then_inc(const_dve, 1)
            layernorm_stats(0)
            dve.memset(vp[0][:], 1.0).then_inc(const_dve, 1)
            dve.memset(vp[1][:], 1.0).then_inc(const_dve, 1)
            dve.memset(mparts[:], 0.0).then_inc(const_dve, 1)
            dve.wait_ge(const_pool, CONST_POOL)
            dve.tensor_copy(identb[:], ident[:]).then_inc(const_dve, 1)
            dve.wait_ge(w_loaded, 16 * n_weights)
            dve.tensor_scalar(bq[:], bq[:], QSCALE, None, ALU.mult).then_inc(const_dve, 1)
            dve.wait_ge(gate_tanh, 1)
            dve.tensor_scalar(bo[:], bo[:], gate[:], None, ALU.mult).then_inc(const_dve, 1)
            if cross:
                dve.tensor_scalar(wT["o"][:], wT["o"][:], gate[:], None, ALU.mult).then_inc(const_dve, 1)
            else:
                dve.tensor_scalar(wm[:, 3], wm[:, 3], gate[:], None, ALU.mult).then_inc(const_dve, 1)
                dve.tensor_scalar(sv[:, 3:4], sv[:, 3:4], gate[:], None, ALU.mult).then_inc(const_dve, 1)
            dve.wait_ge(const_dve, CONST_DVE)

            def job(where, b, op):
                slot, kind = ring[jobs.slot(where, op)], op[0]
                n = jobs.at(where, op)
                if kind == "OT":
                    dve.wait_ge(ring_free, n)
                if kind == "V" and op[1] == 0 and not (isinstance(b, int) and b == 0):
                    dve.wait_ge(v_packed, b * G)
                if kind == "O":
                    dve.wait_ge(xb_ready, b + 1)
                    if not (isinstance(b, int) and b == 0):
                        dve.wait_ge(stored, b * 16)
                if kind == "W" and op[1] == 3 and not (isinstance(b, int) and b == 0):
                    dve.wait_ge(wo_kept, b)
                dve.wait_ge(ring_full, n + 1)
                if kind == "max":
                    _, g, hp, qt, c = op
                    if qt is not None:
                        out, seen = mxp[:, QT * hp + qt, :, c], slot[:, :, 0:CW[c]]
                    else:
                        out = mxp[:, QT * hp:QT * (hp + 1), :, c].rearrange("p q e -> p e q")
                        seen = slot[:, :, 0:QT * CW[c]].rearrange("p e (q k) -> p e q k", q=QT)
                    done = dve.tensor_reduce(out, seen, AX.X, ALU.max)
                elif kind == "OT":
                    g = op[1]
                    seen = slot[:, 0, :].rearrange("p (q j d) -> p q j d", q=QT, j=J)
                    dve.reciprocal(rden[:], seen[:, :, :, D]).then_inc(den_ready, 1)
                    dve.wait_ge(den_ready, b * G + g + 1)
                    done = dve.tensor_tensor(
                        attn[:, :, D * J * g:D * J * (g + 1)].rearrange("p q (j d) -> p q j d", j=J),
                        seen[:, :, :, 0:D], rden[:].unsqueeze(3).broadcast_to([128, QT, J, D]), ALU.mult)
                elif kind == "O":
                    i = 2 * op[1]
                    done = dve.tensor_tensor(xo[:, i:i + 2, :].rearrange("p q c -> p (q c)"),
                                             xres[:, i:i + 2, :].rearrange("p q c -> p (q c)"), slot[:, 0, :], ALU.add)
                elif kind == "V":
                    k0, k1 = st.v_jobs[op[1]]
                    kr = KR[k1 - 1]
                    done = dve.tensor_tensor(
                        vs[0:kr, k0:k1, :],
                        slot[0:kr].rearrange("p a (b n) -> p (a b) n", n=C)[:, 0:k1 - k0, :],
                        bv[0:kr].unsqueeze(1).broadcast_to([kr, k1 - k0, C]), ALU.add)
                elif kind == "lg":
                    done = dve.tensor_tensor(lg[:], gb2[:], slot[0:1, 0, 0:EX], ALU.add)
                elif kind == "W":
                    i = op[1]
                    done = dve.tensor_tensor(wall[:, i].rearrange("p c n -> p (c n)"),
                                             wm[:, i].rearrange("p c n -> p (c n)"), slot[:, 0, :], ALU.add)
                done.then_inc(ring_free, 1)
                if kind == "lg":
                    choose(b, n)

            def max_parts(b, g, maxima):
                k = b * (5 * G) + 5 * g
                at = lambda part: mparts[:, :, 32 + part:128:64]
                dve.wait_ge(ring_free, maxima + 1)
                dve.tensor_reduce(negm[:], mxp[:], AX.X, ALU.max, negate=True).then_inc(m_step, 1)
                dve.wait_ge(m_step, k + 1)
                dve.tensor_copy(at(0), negm[:]).then_inc(m_step, 1)
                dve.wait_ge(m_step, k + 2)
                dve.tensor_tensor(mrest[:], negm[:], at(0), ALU.subtract).then_inc(m_step, 1)
                dve.wait_ge(m_step, k + 3)
                dve.tensor_copy(at(1), mrest[:]).then_inc(m_step, 1)
                dve.wait_ge(m_step, k + 4)
                dve.tensor_tensor(at(2), mrest[:], at(1), ALU.subtract).then_inc(m_step, 1)
                dve.wait_ge(m_step, k + 5)

            def coefficients(b, gates_copied):
                k = b * GATE_STEPS + 15
                dve.wait_ge(tile_done, gates_copied + 1)
                dve.tensor_tensor(gsel[:], onehot[:], gsb[:], ALU.mult).then_inc(gate_step, 1)
                dve.wait_ge(gate_step, k + 1)
                dve.tensor_reduce(csum[:], gsel[:], AX.X, ALU.add).then_inc(gate_step, 1)
                dve.wait_ge(gate_step, k + 2)
                dve.tensor_scalar(coef[:], sv[:], csum[:], None, ALU.mult).then_inc(gate_step, 1)

            def choose(b, n):
                k = [b * GATE_STEPS]

                def done(op):
                    op.then_inc(gate_step, 1)
                    k[0] = k[0] + 1
                    dve.wait_ge(gate_step, k[0])

                dve.wait_ge(ring_free, n + 1)
                for r, row in ((0, lg), (1, lg2)):
                    if r:
                        done(dve.scalar_tensor_tensor(lg2[:], pick[:, 0, :], -3.0e38, lg[:], ALU.mult, ALU.add))
                    done(dve.tensor_reduce(top[:, 2 * r:2 * r + 1], row[:], AX.X, ALU.max))
                    done(dve.scalar_tensor_tensor(cand[:, r, :], row[:], top[:, 2 * r:2 * r + 1], prio[:],
                                                  ALU.is_ge, ALU.mult))
                    done(dve.tensor_reduce(top[:, 2 * r + 1:2 * r + 2], cand[:, r, :], AX.X, ALU.max))
                    done(dve.tensor_scalar(pick[:, r, :], cand[:, r, :], top[:, 2 * r + 1:2 * r + 2], None, ALU.is_equal))
                done(dve.tensor_tensor(top[:, 4:5], top[:, 2:3], top[:, 0:1], ALU.subtract))
                dve.wait_ge(gate_exp, b + 1)
                done(dve.tensor_scalar(top[:, 6:7], top[:, 5:6], 1.0, None, ALU.add))
                done(dve.reciprocal(top[:, 7:8], top[:, 6:7]))
                done(dve.tensor_scalar(gates[:, 0, :], pick[:, 1, :], top[:, 5:6], None, ALU.mult))
                done(dve.tensor_tensor(gates[:, 0, :], gates[:, 0, :], pick[:, 0, :], ALU.add))
                done(dve.tensor_scalar(gates[:, 1, :], gates[:, 0, :], top[:, 7:8], None, ALU.mult))

            def one(where, b, op):
                if op in jobs.uses(where):
                    job(where, b, op)
                elif op[0] == "MS":
                    max_parts(b, op[1], jobs.at(where, st.maxima(op[1])[-1]))
                elif op[0] == "coef":
                    coefficients(b, tiles.at(where, ("gb",)))
                elif op[0] == "stats":
                    layernorm_stats(b)

            for b, where in ((-2, "opening"), (-1, "prologue")):
                for op in st.plans[where]:
                    one(where, st.batch_of(b, op), op)
                    if op == ("Q", 1) or op in LAST_K.values():
                        split_parts(dve, dve_past, 0, -1 if op[0] == "Q" else op[1],
                                    lambda made: tiles.at("prologue", made))

            def body(b):
                for op in st.plans[kind_of(b)]:
                    one(b, st.batch_of(b, op), op)

            over_batches(dve, body)
            for op in st.plans["tail"]:
                one("tail", B - 1, op)

        @block.gpsimd
        def _(pool):
            pool.memset(ident[:], 0.0).then_inc(const_pool, 1)
            pool.wait_ge(const_pool, 1)
            pool.affine_select(out=ident[:], in_=ident[:], compare_op=ALU.not_equal, fill=1.0, base=0,
                               pattern=[[-1, 128]], channel_multiplier=1).then_inc(const_pool, 1)
            pool.wait_ge(const_pool, 2)
            pool.memset(nhalf[:], -0.5).then_inc(const_pool, 1)
            pool.wait_ge(const_pool, 3)
            if not cross:
                for e in range(EX):
                    pool.memset(prio[:, e:e + 1], float(EX - e)).then_inc(const_pool, 1)
                    pool.wait_ge(const_pool, 4 + e)
                pool.memset(ones[:], 1.0).then_inc(const_pool, 1)
                pool.wait_ge(const_pool, 4 + EX)
                pool.memset(euler[:], 2.718281828459045).then_inc(const_pool, 1)
                pool.wait_ge(const_pool, 5 + EX)
                pool.memset(onehot[:], 1.0).then_inc(const_pool, 1)
                pool.wait_ge(const_pool, 6 + EX)
                pool.affine_select(out=onehot[:], in_=onehot[:], compare_op=ALU.is_ge, fill=0.0, base=0,
                                   pattern=[[-RANK, EX]], channel_multiplier=1).then_inc(const_pool, 1)
                pool.wait_ge(const_pool, 7 + EX)
                pool.affine_select(out=onehot[:], in_=onehot[:], compare_op=ALU.is_ge, fill=0.0, base=RANK - 1,
                                   pattern=[[RANK, EX]], channel_multiplier=-1).then_inc(const_pool, 1)
                pool.wait_ge(const_pool, 8 + EX)
            def fixed_rows(g):
                for i, (rows, value) in enumerate(((kst[96:128, g, 0:2, :], 1.0), (qst[32:64, g, 2:4, :], 0.0),
                                                   (kst[32:64, g, 2:4, :], 0.0), (kst[32:35, g, 2:4, :], 1.0))):
                    pool.memset(rows, value).then_inc(rows_set, 1)
                    pool.wait_ge(rows_set, 4 * g + i + 1)

            def layernorm(b):
                k = b * 3
                pool.wait_ge(stats_done, b + 1)
                pool.sem_inc(pool_past, 1)
                pool.tensor_scalar(veps[:], mv[:, :, 1], EPS, None, ALU.add).then_inc(ln_step, 1)
                pool.tensor_scalar(nmean[:], mv[:, :, 0], -1.0, None, ALU.mult).then_inc(ln_step, 1)
                pool.wait_ge(ln_step, k + 2)
                pool.sem_inc(pool_past, 1)
                pool.tensor_tensor(rstd[:], veps[:], nhalf[:], ALU.pow).then_inc(ln_step, 1)
                pool.wait_ge(ln_step, k + 3)
                pool.sem_inc(pool_past, 1)
                for qt in range(QT):
                    last = pool.tensor_scalar(xt[:, qt, :], xt[:, qt, :], nmean[:, qt:qt + 1], rstd[:, qt:qt + 1],
                                              ALU.add, ALU.mult)
                last.then_inc(xhat_ready, 1)

            def pack_v(b, g, number):
                if number is not None:
                    pool.wait_ge(ring_free, number(LAST_V) + 1)
                    pool.sem_inc(pool_past, 1)
                if not (isinstance(b, int) and b == 0 and g < 2):
                    pool.wait_ge(pv_done, b * STEPS + (g - 1) * NK)
                    pool.sem_inc(pool_past, 1)
                for j in range(J):
                    last = pool.tensor_copy(vp[g % 2][:, :, VW * j:VW * j + D],
                                            vs[:, :, D * (J * g + j):D * (J * g + j + 1)])
                last.then_inc(v_packed, 1)

            def residual(b):
                pool.wait_ge(xres_loaded, b * 16 + 16)
                pool.sem_inc(pool_past, 1)
                for qt in range(QT):
                    last = pool.tensor_tensor(xres[:, qt, :], xres[:, qt, :], bo[:], ALU.add)
                last.then_inc(xb_ready, 1)

            def gate_exponential(b):
                pool.wait_ge(gate_step, b * GATE_STEPS + 10)
                pool.sem_inc(pool_past, 1)
                pool.tensor_tensor(top[:, 5:6], euler[:], top[:, 4:5], ALU.pow).then_inc(gate_exp, 1)

            def scale_u(b):
                pool.wait_ge(gate_step, b * GATE_STEPS + 18)
                pool.sem_inc(pool_past, 1)
                for i in range(4):
                    last = pool.tensor_scalar(uc[:, i, :], uT[:, i, :], coef[:, i:i + 1], None, ALU.mult)
                last.then_inc(uc_ready, 1)

            def keep_wo(b, number):
                pool.wait_ge(ring_free, number + 1)
                pool.sem_inc(pool_past, 1)
                pool.tensor_copy(wT["o"][:], wall[:, 3]).then_inc(wo_kept, 1)

            job_pro = lambda op: jobs.at("prologue", op)
            layernorm(0)
            pool.wait_ge(xhat_ready, 1)
            fixed_rows(0)
            pool.wait_ge(const_dve, CONST_DVE)
            if not cross:
                gate_exponential(0)
                scale_u(0)
            layernorm(1)
            pool.wait_ge(xhat_ready, 2)
            for g in range(1, G):
                fixed_rows(g)
            if not cross:
                gate_exponential(1)
            pack_v(0, 0, job_pro)
            if not cross:
                scale_u(1)

            def body(b):
                post, prep, ahead = flags(b)
                tile_here = lambda op: tiles.at(b, op)
                job_here = lambda op: jobs.at(b, op)
                if post:
                    residual(b - 1)
                pack_v(b, 1, None)
                if cross:
                    if prep:
                        split_parts(pool, pool_past, b + 1, -1, tile_here)
                        split_parts(pool, pool_past, b + 1, 0, tile_here)
                    pack_v(b, 2, None)
                    if prep:
                        split_parts(pool, pool_past, b + 1, 1, tile_here)
                        split_parts(pool, pool_past, b + 1, 2, tile_here)
                        split_parts(pool, pool_past, b + 1, 3, tile_here)
                    pack_v(b, 3, None)
                    if ahead:
                        layernorm(b + 2)
                    if prep:
                        pack_v(b + 1, 0, job_here)
                else:
                    if prep:
                        split_parts(pool, pool_past, b + 1, -1, tile_here)
                    pack_v(b, 2, None)
                    if prep:
                        split_parts(pool, pool_past, b + 1, 0, tile_here)
                    keep_wo(b, jobs.at(b, ("O", 1)) if post else job_pro(("W", 3)))
                    pack_v(b, 3, None)
                    if ahead:
                        layernorm(b + 2)
                        gate_exponential(b + 2)
                    if prep:
                        pack_v(b + 1, 0, job_here)
                    if ahead:
                        scale_u(b + 2)

            over_batches(pool, body)
            residual(B - 1)


def flamingo_layer(nc, x, ctxT, wx, we, y, out):
    def parts(name, n):
        return nc.dram_tensor(name, (2 * G, len(TERMS), D, 2, n), BF16, kind="Internal").ap()

    with ExitStack() as sems:
        run_stage(nc, Stage(True), sems, x, y, ctxT, wx, (parts("cross_q", T), parts("cross_k", KEYS)), "cross")
        run_stage(nc, Stage(False), sems, y, out, None, we, (parts("expert_q", T), parts("expert_k", T)), "expert")


def kernel(**inputs):
    import numpy as np
    import concourse.bacc as bacc
    from concourse.bass_utils import run_bass_kernel_spmd

    a = {n: np.asarray(v) for n, v in inputs.items()}

    def rows(v, n=128):
        return np.broadcast_to(v.reshape(1, -1), (n, v.size))

    def column(v):
        return v.reshape(-1, 128).T

    def paired(v):
        shape = v.shape[:-1]
        v = v.reshape(*shape, 2 * G, 2, D)
        return np.moveaxis(v, -2, -3).reshape(*shape, C)

    f, c = "L0_ffn_", "L0_xattn_"
    names = ("q", "k", "v", "o")
    data = {"x": a["x"], "ctxT": a["ctx_1024"].transpose(0, 2, 1)}
    wx = {"w" + n: a[c + "W" + n].T for n in names}
    wx |= {"bv": rows(a[c + "bv"]), "bo": rows(a[c + "bo"]),
           "gate": rows(a["g_xattn"])}
    we = {"w" + n: a[f + n + "Wm"].T for n in names}
    for d, bq, bk in ((wx, a[c + "bq"], a[c + "bk"]), (we, a[f + "qb"], a[f + "kb"])):
        d |= {"wq": paired(d["wq"]), "wk": paired(d["wk"]), "bq": column(paired(bq)), "bk": column(paired(bk))}
    we |= {"u": np.stack([(paired if n in "qk" else np.asarray)(a[f + n + "U"].transpose(0, 2, 1).reshape(EX * RANK, C))
                          for n in names]),
           "v": np.stack([a[f + n + "V"].reshape(EX * RANK, C) for n in names]),
           "s": np.stack([a[f + n + "S"].reshape(EX * RANK) for n in names], 1),
           "bv": rows(a[f + "vb"]), "bo": rows(a[f + "ob"]),
           "gate": rows(a["g_ffn"]), "gw1": a[f + "gw1"].T, "gw2": a[f + "gw2"].T,
           "gb1": a[f + "gb1"].reshape(-1, 1), "gb2": a[f + "gb2"].reshape(1, -1)}
    data |= {"x_" + n: v for n, v in wx.items()} | {"e_" + n: v for n, v in we.items()}

    nc = bacc.Bacc("TRN2", target_bir_lowering=False, num_devices=1)
    arrays, aps = {}, {}
    for name, v in data.items():
        arrays[f"in_{name}"] = np.ascontiguousarray(v)
        aps[name] = nc.dram_tensor(f"in_{name}", v.shape, mybir.dt.from_np(v.dtype), kind="ExternalInput").ap()
    y = nc.dram_tensor("after_cross", (B, T, C), F32, kind="Internal").ap()
    out = nc.dram_tensor("out", (B, T, C), F32, kind="ExternalOutput").ap()
    flamingo_layer(nc, aps["x"], aps["ctxT"], {n: aps["x_" + n] for n in wx}, {n: aps["e_" + n] for n in we}, y, out)
    r = run_bass_kernel_spmd(nc, [arrays], core_ids=[0])
    return r.results[0]["out"]
```
